# Optimizing a Trainium2 kernel written in Bass

```python
import numpy as np
import jax
import jax.numpy as jnp

def _softmax(x, axis=-1):
    return jax.nn.softmax(x, axis=axis)

def _gelu(x):
    return jax.nn.gelu(x, approximate=True)

def _silu(x):
    return jax.nn.silu(x)

def _sigmoid(x):
    return jax.nn.sigmoid(x)

def _layernorm(x, axis=-1, eps=1e-05):
    m = jnp.mean(x, axis=axis, keepdims=True)
    v = jnp.var(x, axis=axis, keepdims=True)
    return (x - m) / jnp.sqrt(v + eps)

def _scatter_add(tgt, idx, src, axis=0):
    return tgt.at[idx].add(src)

def _segment_sum(src, seg, n):
    return jax.ops.segment_sum(src, seg, n)
kernel_name = 'mk_adaln_d1_jaxref_r8_2b9be3'

def setup_inputs(seed: int=0):
    np.random.seed(seed)
    _w = jnp.asarray

    def _L0_attn_setup():
        import jax, jax.numpy as jnp
        import numpy as np
        HEADS = 16

        def _binarize(W):
            alpha = jnp.mean(jnp.abs(W), axis=tuple(range(1, W.ndim)), keepdims=True)
            B = W + jax.lax.stop_gradient(jnp.sign(W) - W)
            return alpha * B

        def _binlinear(x, W, b):
            Wb = _binarize(W)
            return jnp.einsum('btc,oc->bto', x, Wb) + b
        key = jax.random.key(seed)
        ks = jax.random.split(key, 9)
        dim = 128
        B, T = (4, 256)
        inp = {'x': jax.random.normal(ks[0], (B, T, dim), jnp.float32), 'Wq': jax.random.normal(ks[1], (dim, dim), jnp.float32) * 0.02, 'bq': jax.random.normal(ks[2], (dim,), jnp.float32) * 0.02, 'Wk': jax.random.normal(ks[3], (dim, dim), jnp.float32) * 0.02, 'bk': jax.random.normal(ks[4], (dim,), jnp.float32) * 0.02, 'Wv': jax.random.normal(ks[5], (dim, dim), jnp.float32) * 0.02, 'bv': jax.random.normal(ks[6], (dim,), jnp.float32) * 0.02, 'Wp': jax.random.normal(ks[7], (dim, dim), jnp.float32) * 0.02, 'bp': jax.random.normal(ks[8], (dim,), jnp.float32) * 0.02}
        return inp
    _L0_attn_in = _L0_attn_setup()

    def _L0_ffn_setup():
        import jax, jax.numpy as jnp
        import numpy as np
        B, S, H = (2, 256, 128)
        E_ROUTED = 8
        TOP_K = 2
        I = 256
        key = jax.random.key(seed)
        ks = jax.random.split(key, 9)
        s = 0.02
        return {'x': jax.random.normal(ks[0], (B, S, H), dtype=jnp.float32), 'shared_gate': jax.random.normal(ks[1], (I, H), dtype=jnp.float32) * s, 'shared_up': jax.random.normal(ks[2], (I, H), dtype=jnp.float32) * s, 'shared_down': jax.random.normal(ks[3], (H, I), dtype=jnp.float32) * s, 'gate_w': jax.random.normal(ks[4], (E_ROUTED, H, I), dtype=jnp.float32) * s, 'up_w': jax.random.normal(ks[5], (E_ROUTED, H, I), dtype=jnp.float32) * s, 'down_w': jax.random.normal(ks[6], (E_ROUTED, I, H), dtype=jnp.float32) * s, 'router_w': jax.random.normal(ks[7], (E_ROUTED, H), dtype=jnp.float32) * s, 'routing_bias': jnp.zeros((E_ROUTED,), dtype=jnp.float32)}
    _L0_ffn_in = _L0_ffn_setup()
    _L0_c = _w((lambda *s: np.random.randn(*s).astype(np.float32) * 0.05)(8, 128))
    _L0_wmod = _w((lambda *s: np.random.randn(*s).astype(np.float32) * 0.05)(128, 6 * 128) * 128 ** (-0.5))
    _d = {'L0_attn_x': _L0_attn_in['x'], 'L0_attn_Wq': _L0_attn_in['Wq'], 'L0_attn_bq': _L0_attn_in['bq'], 'L0_attn_Wk': _L0_attn_in['Wk'], 'L0_attn_bk': _L0_attn_in['bk'], 'L0_attn_Wv': _L0_attn_in['Wv'], 'L0_attn_bv': _L0_attn_in['bv'], 'L0_attn_Wp': _L0_attn_in['Wp'], 'L0_attn_bp': _L0_attn_in['bp'], 'L0_ffn_shared_gate': _L0_ffn_in['shared_gate'], 'L0_ffn_shared_up': _L0_ffn_in['shared_up'], 'L0_ffn_shared_down': _L0_ffn_in['shared_down'], 'L0_ffn_gate_w': _L0_ffn_in['gate_w'], 'L0_ffn_up_w': _L0_ffn_in['up_w'], 'L0_ffn_down_w': _L0_ffn_in['down_w'], 'L0_ffn_router_w': _L0_ffn_in['router_w'], 'L0_ffn_routing_bias': _L0_ffn_in['routing_bias'], 'L0_c': _L0_c, 'L0_wmod': _L0_wmod}
    _x0 = _d['L0_attn_x']
    _d['L0_attn_x'] = jax.random.normal(jax.random.fold_in(jax.random.key(seed), 1), (8, 512, 128), dtype=_x0.dtype)
    del _x0
    return _d

def reference(L0_attn_x, L0_attn_Wq, L0_attn_bq, L0_attn_Wk, L0_attn_bk, L0_attn_Wv, L0_attn_bv, L0_attn_Wp, L0_attn_bp, L0_ffn_shared_gate, L0_ffn_shared_up, L0_ffn_shared_down, L0_ffn_gate_w, L0_ffn_up_w, L0_ffn_down_w, L0_ffn_router_w, L0_ffn_routing_bias, L0_c, L0_wmod):

    def _L0_attn_ref(x, Wq, bq, Wk, bk, Wv, bv, Wp, bp):
        import jax, jax.numpy as jnp
        import numpy as np
        HEADS = 16

        def _binarize(W):
            alpha = jnp.mean(jnp.abs(W), axis=tuple(range(1, W.ndim)), keepdims=True)
            B = W + jax.lax.stop_gradient(jnp.sign(W) - W)
            return alpha * B

        def _binlinear(x, W, b):
            Wb = _binarize(W)
            return jnp.einsum('btc,oc->bto', x, Wb) + b
        B, T, C = x.shape
        H = HEADS
        Dh = C // H
        scale = Dh ** (-0.5)

        def split_heads(t):
            return t.reshape(B, T, H, Dh).transpose(0, 2, 1, 3)
        q = split_heads(_binlinear(x, Wq, bq))
        k = split_heads(_binlinear(x, Wk, bk))
        v = split_heads(_binlinear(x, Wv, bv))
        att = jnp.einsum('bhtd,bhsd->bhts', q, k) * scale
        att = jax.nn.softmax(att, axis=-1)
        y = jnp.einsum('bhts,bhsd->bhtd', att, v)
        y = y.transpose(0, 2, 1, 3).reshape(B, T, C)
        return _binlinear(y, Wp, bp)

    def _L0_ffn_ref(x, shared_gate, shared_up, shared_down, gate_w, up_w, down_w, router_w, routing_bias):
        import jax, jax.numpy as jnp
        import numpy as np
        B, S, H = (2, 256, 128)
        E_ROUTED = 8
        TOP_K = 2
        I = 256
        b, s, h = x.shape
        shared = jnp.einsum('bsi,hi->bsh', jax.nn.silu(jnp.einsum('bsh,ih->bsi', x, shared_gate)) * jnp.einsum('bsh,ih->bsi', x, shared_up), shared_down)
        logits = jnp.einsum('bsh,eh->bse', x, router_w) + routing_bias
        probs = jax.nn.sigmoid(logits)
        scores, indices = jax.lax.top_k(probs, TOP_K)
        scores = scores / jnp.sum(scores, axis=-1, keepdims=True)
        t = b * s
        xf = x.reshape(t, h)
        idx = indices.reshape(t, TOP_K)
        sc = scores.reshape(t, TOP_K)
        w = jnp.zeros((t, E_ROUTED), dtype=x.dtype)
        w = w.at[jnp.arange(t)[:, None], idx].add(sc)
        g = jax.nn.silu(jnp.einsum('th,ehi->tei', xf, gate_w))
        u = jnp.einsum('th,ehi->tei', xf, up_w)
        combined = jnp.einsum('tei,eih,te->th', g * u, down_w, w)
        return shared + combined.reshape(b, s, h)
    x = L0_attn_x
    mod = (_silu(L0_c) @ L0_wmod).reshape(L0_c.shape[0], 6, 1, -1)
    sa, ca, ga, sb, cb, gb = (mod[:, 0], mod[:, 1], mod[:, 2], mod[:, 3], mod[:, 4], mod[:, 5])
    ga = (2 * (ga >= 0) - 1) * jnp.maximum(jnp.abs(ga), 0.25)
    gb = (2 * (gb >= 0) - 1) * jnp.maximum(jnp.abs(gb), 0.25)
    h = _layernorm(x, axis=-1) * (1 + ca) + sa
    x = x + ga * _L0_attn_ref(h, L0_attn_Wq, L0_attn_bq, L0_attn_Wk, L0_attn_bk, L0_attn_Wv, L0_attn_bv, L0_attn_Wp, L0_attn_bp)
    h = _layernorm(x, axis=-1) * (1 + cb) + sb
    x = x + gb * _L0_ffn_ref(h, L0_ffn_shared_gate, L0_ffn_shared_up, L0_ffn_shared_down, L0_ffn_gate_w, L0_ffn_up_w, L0_ffn_down_w, L0_ffn_router_w, L0_ffn_routing_bias)
    return x

_drawn_inputs = setup_inputs


def setup_inputs(seed=0):
    import zlib

    import numpy as np

    out = dict(_drawn_inputs(seed))
    spreads = {'L0_ffn_routing_bias': (0.0, 0.8)}
    factors = {'L0_attn_Wq': 8.0,
     'L0_attn_bq': 8.0,
     'L0_attn_Wk': 8.0,
     'L0_attn_bk': 8.0,
     'L0_attn_Wv': 8.0,
     'L0_attn_bv': 8.0,
     'L0_attn_Wp': 8.0,
     'L0_attn_bp': 8.0,
     'L0_ffn_shared_gate': 8.0,
     'L0_ffn_shared_up': 8.0,
     'L0_ffn_shared_down': 8.0,
     'L0_ffn_gate_w': 8.0,
     'L0_ffn_up_w': 8.0,
     'L0_ffn_down_w': 8.0,
     'L0_ffn_router_w': 8.0,
     'L0_c': 8.0,
     'L0_wmod': 8.0}
    for name, (base, spread) in spreads.items():
        noise = np.random.default_rng([zlib.crc32(name.encode()), seed]).standard_normal(out[name].shape)
        drawn = base * np.exp(spread * noise) if base else spread * noise
        out[name] = jnp.asarray(drawn.astype(out[name].dtype))
    for name, factor in factors.items():
        out[name] = (out[name] * factor).astype(out[name].dtype)
    return out
```

```python
from contextlib import ExitStack

import concourse.bass as bass
from concourse import mybir

ALU = mybir.AluOpType
ACT = mybir.ActivationFunctionType
AX_X = mybir.AxisListType.X
F32 = mybir.dt.float32
BF16 = mybir.dt.bfloat16

P = 128
B, T, C = 8, 512, 128
H = 16
DH = C // H
TT = T // P
HG = 4
G = H // HG
SLOTS = G * TT
E, I = 8, 256
IC = I // P
PARTS = 3
PROD = PARTS * PARTS * DH
MROW = 96
SCALE = float(DH) ** -0.5
EPS = 1e-5
U32 = mybir.dt.uint32
I32 = mybir.dt.int32
TOKENS = B * T
K_TOP = 2
REC = C + 2
REGION = TOKENS + P
UNITS = K_TOP * TOKENS // P + E
RING = 8
FAR = 1 << 20


def adaln_block(nc: bass.Bass, x, Wq, bq, Wk, bk, Wv, bv, Wp, bp, sh_gate, sh_up, sh_down,
                gate_w, up_w, down_w, router_w, routing_bias, c, wmod, out):
    ctx = ExitStack()
    with ctx:
        def sb(name, shape, dt=F32):
            return ctx.enter_context(nc.sbuf_tensor(name, shape, dt))

        def psum(name, shape):
            return ctx.enter_context(nc.psum_tensor(name, shape, F32))

        def sem(name):
            return ctx.enter_context(nc.semaphore(name))

        st_bank = [psum(f"st{i}", [P, T]) for i in range(2)]
        mx_bank = [psum(f"mx{i}", [P, 2, T]) for i in range(2)]
        pv_bank = psum("pv", [P, T])
        misc = psum("misc", [P, T])
        misc_bf = misc[:, :].bitcast(BF16)

        qs = [sb(f"qs{i}", [P, H, T], BF16) for i in range(2)]
        ks = [sb(f"ks{i}", [P, H, T], BF16) for i in range(2)]
        vs = [sb(f"vs{i}", [P, TT, H, 32]) for i in range(2)]
        pt = [sb(f"pt{i}", [P, HG, T]) for i in range(2)]
        gate_up = qs[0][:].rearrange("p h t -> p (h t)").bitcast(F32).rearrange("p (e i) -> p e i", e=E)
        down = ks[0][:].rearrange("p h t -> p (h t)").bitcast(F32)[:, 0:E * I].rearrange("p (e j c) -> p e j c", e=E, j=IC)
        scratch = [b[:].rearrange("p h t -> p (h t)") for b in pt]
        w_sgn = scratch[0][:, 0:4 * C].rearrange("p (i c) -> p i c", c=C)
        w_neg = scratch[0][:, 4 * C:8 * C].rearrange("p (i c) -> p i c", c=C)
        nat = scratch[0][:, 8 * C:14 * C].rearrange("p (j c) -> p j c", c=C)
        silu_bc = scratch[1][:, 0:B * P].rearrange("p (b q) -> p b q", q=P)
        gate_sign = scratch[1][:, B * P:2 * B * P].rearrange("p (b c) -> p b c", c=C)
        ident = sb("ident", [P, P])
        ident_bf = sb("ident_bf", [P, P], BF16)
        w_nat = sb("w_nat", [P, 4, C])
        alpha = sb("alpha", [P, 4])
        wT = sb("wT", [P, 4, C])
        bias_qkv = sb("bias_qkv", [P, 3])
        silu_T = sb("silu_T", [P, B])
        wmod_sb = sb("wmod_sb", [P, 6 * C])
        mod_T = sb("mod_T", [P, 2, B])
        bp_bc = sb("bp_bc", [P, C])
        ga_bc = sb("ga_bc", [P, B, C])
        gb_bc = sb("gb_bc", [P, B, C])
        sb_bc = sb("sb_bc", [P, B, C])
        cb_bc = sb("cb_bc", [P, B, C])
        x_in = sb("x_in", [P, TT, C])
        x_ep = sb("x_ep", [P, TT, C])
        ln1 = sb("ln1", [P, TT, C])
        hT = sb("hT", [P, T])
        qk_f = [sb(f"qk_f{i}", [P, T]) for i in range(2)]
        qk_r = sb("qk_r", [P, T])
        qk_parts = [sb(f"qk_parts{i}", [P, PARTS, T], BF16) for i in range(2)]
        neg_max = [sb(f"neg_max{i}", [P, HG, TT]) for i in range(2)]
        m_rest = sb("m_rest", [P, HG * TT])
        m_parts = sb("m_parts", [P, PARTS, HG * TT], BF16)
        m_rows = [sb(f"m_rows{i}", [PARTS * HG * TT, P], BF16) for i in range(2)]
        y_strips = sb("y_strips", [P, T])
        y_rden = sb("y_rden", [P, TT, HG])
        y_tok = sb("y_tok", [P, TT, C])
        yT = sb("yT", [P, T])
        wp_ga = sb("wp_ga", [P, C])
        bp_ga = sb("bp_ga", [P, C])
        c_nat = sb("c_nat", [B, C])
        h2T = sb("h2T", [P, B * T])
        h2T_now = sb("h2T_now", [P, T])
        router_nat = sb("router_nat", [E, C])
        router_T = sb("router_T", [P, E])
        router_bias = sb("router_bias", [P, E])
        shared_w = sb("shared_w", [P, 4, P])
        shared_down = sb("shared_down", [P, IC, C])
        expert_no = sb("expert_no", [P, E])
        expert_no_i = sb("expert_no_i", [P, E], I32)
        before = sb("before", [P, P], BF16)
        ones_bf = sb("ones_bf", [P, P], BF16)
        logits = sb("logits", [P, TT, E])
        probs = sb("probs", [P, TT, E])
        top_p = sb("top_p", [P, TT, 8])
        top_e = sb("top_e", [P, TT, 8], U32)
        top_ef = sb("top_ef", [P, TT, K_TOP])
        p_sum = sb("p_sum", [P, TT])
        p_rsum = sb("p_rsum", [P, TT])
        chosen = sb("chosen", [P, K_TOP, TT, E])
        marks = sb("marks", [P, TT + 1, E], BF16)
        place = sb("place", [P, TT, E])
        next_row = [sb(f"next_row{i}", [P, E]) for i in range(2)]
        picked = sb("picked", [P, K_TOP, TT, E])
        row_f = sb("row_f", [P, K_TOP, TT])
        row_u = sb("row_u", [P, K_TOP, TT], U32)
        home = sb("home", [P, K_TOP, TT])
        stats1_sb = sb("stats1_sb", [P, TT, 6])
        mv1 = sb("mv1", [P, TT, 2])
        rstd1 = sb("rstd1", [P, TT])
        stats2_sb = sb("stats2_sb", [P, TT, 6])
        mv2 = sb("mv2", [P, TT, 2])
        rstd2 = sb("rstd2", [P, TT])
        ve1 = sb("ve1", [P, TT])
        ve2 = sb("ve2", [P, TT])
        minus_half = sb("minus_half", [P, TT])
        ln2 = sb("ln2", [P, TT, C])
        rec = [sb(f"rec{i}", [P, K_TOP, TT, REC]) for i in range(2)]
        x1 = sb("x1", [P, B * TT, C])

        pad_row = sb("pad_row", [P, REC])
        first_row = sb("first_row", [P, E])
        unit_start = sb("unit_start", [P, UNITS])
        earlier = sb("earlier", [P, E, E])
        padded = sb("padded", [P, E])
        padded_i = sb("padded_i", [P, E], I32)
        region_end = sb("region_end", [P, E])
        skip = sb("skip", [P, E])
        entered = sb("entered", [P, UNITS, E])
        skipped = sb("skipped", [P, UNITS, E])
        unit_f = sb("unit_f", [P, 2, UNITS])
        unit_row = sb("unit_row", [P, UNITS], I32)
        digit = sb("digit", [P, RING])
        digits = sb("digits", [P, UNITS // RING, RING])
        packed_f = sb("packed_f", [P, UNITS // RING])
        turn_experts = sb("turn_experts", [P, UNITS // RING], I32)
        end_row = sb("end_row", [P, E], I32)
        silu_s = pt[0][:, 0:IC, :]
        act_s = pt[1][:].rearrange("p (b j) t -> p b j t", b=2)
        gated = pt[0][:, 2, :].rearrange("p (t c) -> p t c", t=TT)
        odd_q, odd_k = (b[1][:].rearrange("p h t -> p (h t)").bitcast(F32) for b in (qs, ks))
        xu = [odd_k[:, i * REC:(i + 1) * REC] for i in range(RING)]
        y_u = [odd_q[:, i * C:(i + 1) * C] for i in range(RING)]
        w_u = [odd_q[:, RING * C + i:RING * C + i + 1] for i in range(RING)]
        home_u = sb("home_u", [P, RING], U32)
        unit_a = vs[0][:].rearrange("p t h d -> p (t h d)")
        unit_b = vs[1][:].rearrange("p t h d -> p (t h d)")
        xuT = [unit_a[:, i * P:(i + 1) * P] for i in range(2)]
        silu_u = [unit_a[:, 2 * P + i * I:2 * P + (i + 1) * I] for i in range(2)]
        act_u = [unit_b[:, i * I:(i + 1) * I] for i in range(2)]
        actT_u = [unit_b[:, (2 + i) * I:(3 + i) * I] for i in range(2)]
        results = [[(odd_q, odd_k)[b // (B // 2)][:, (2 * (b % (B // 2)) + k) * T:(2 * (b % (B // 2)) + k + 1) * T]
                    .rearrange("p (t c) -> p t c", t=TT) for k in range(K_TOP)] for b in range(B)]

        q_dram = nc.dram_tensor("q_parts", (PARTS, DH, H, T), BF16).ap()
        routed_dram = nc.dram_tensor("routed", (E * REGION + P, REC), F32).ap()
        result_dram = nc.dram_tensor("results", (K_TOP * TOKENS, C), F32).ap()
        k_dram = nc.dram_tensor("k_parts", (PARTS, DH, H, T), BF16).ap()

        w_loaded = sem("w_loaded")
        small_loaded = sem("small_loaded")
        c_loaded = sem("c_loaded")
        pool_ready = sem("pool_ready")
        consts_ready = sem("consts_ready")
        setup_dve = sem("setup_dve")
        setup_pe = sem("setup_pe")
        setup_act = sem("setup_act")
        setup_pool = sem("setup_pool")
        x_in_loaded = sem("x_in_loaded")
        x_ep_loaded = sem("x_ep_loaded")
        stats1_ready = sem("stats1_ready")
        rstd1_ready = sem("rstd1_ready")
        ln1_ready = sem("ln1_ready")
        hT_ready = sem("hT_ready")
        qk_ready = sem("qk_ready")
        rest_ready = sem("rest_ready")
        parts_ready = sem("parts_ready")
        q_stored = sem("q_stored")
        k_stored = sem("k_stored")
        stacks_cleared = sem("stacks_cleared")
        var1_ready = sem("var1_ready")
        var2_ready = sem("var2_ready")
        m_chain = sem("m_chain")
        h2_chain = sem("h2_chain")
        home_ready = sem("home_ready")
        home_chain = sem("home_chain")
        sig_exp = sem("sig_exp")
        route_chain = sem("route_chain")
        marks_ready = sem("marks_ready")
        rank_chain = sem("rank_chain")
        rows_ready = sem("rows_ready")
        weights_ready = sem("weights_ready")
        scattered = sem("scattered")
        rows_free = sem("rows_free")
        shared_loaded = sem("shared_loaded")
        routed_loaded = sem("routed_loaded")
        bp_ga_ready = sem("bp_ga_ready")
        stack_loaded = [sem(f"stack_loaded{i}") for i in range(2)]
        v_ready = sem("v_ready")
        misc_full = sem("misc_full")
        misc_free = sem("misc_free")
        mx_full = sem("mx_full")
        mx_free = sem("mx_free")
        m_split = sem("m_split")
        m_row_ready = sem("m_row_ready")
        m_row_loaded = [sem(f"m_row_loaded{i}") for i in range(2)]
        st_full = sem("st_full")
        exp_done = sem("exp_done")
        pv_done = sem("pv_done")
        y_evacuated = sem("y_evacuated")
        rden_ready = sem("rden_ready")
        y_tok_ready = sem("y_tok_ready")
        yT_ready = sem("yT_ready")
        xres_ready = sem("xres_ready")
        wp_ga_ready = sem("wp_ga_ready")
        x1_ready = sem("x1_ready")
        stats_chain = sem("stats_chain")
        stats2_ready = sem("stats2_ready")
        rstd2_ready = sem("rstd2_ready")
        ln2_ready = sem("ln2_ready")
        h2_ready = sem("h2_ready")
        out_stored = sem("out_stored")
        s_full = sem("s_full")
        s_silu = sem("s_silu")
        s_act = sem("s_act")
        s_down = sem("s_down")
        s_gated = sem("s_gated")
        s_out = sem("s_out")
        table_chain = sem("table_chain")
        tables_ready = sem("tables_ready")
        padding_written = sem("padding_written")
        xu_loaded = [sem(f"xu_loaded{i}") for i in range(RING)]
        xu_read = sem("xu_read")
        xuT_full = sem("xuT_full")
        xuT_ready = sem("xuT_ready")
        gu_full = sem("gu_full")
        silu_ready = sem("silu_ready")
        act_ready = sem("act_ready")
        actT_full = sem("actT_full")
        actT_ready = sem("actT_ready")
        yu_full = sem("yu_full")
        yu_ready = sem("yu_ready")
        yu_sent = [sem(f"yu_sent{i}") for i in range(RING)]
        results_loaded = [sem(f"results_loaded{i}") for i in range(B)]
        results_added = sem("results_added")
        out_ready = sem("out_ready")
        out_chain = sem("out_chain")
        pad_ready = sem("pad_ready")
        stats1_chain = sem("stats1_chain")
        stats2_chain = sem("stats2_chain")
        v_cleared = sem("v_cleared")
        bc_full = sem("bc_full")
        bc_free = sem("bc_free")
        gate_chain = sem("gate_chain")
        gates_ready = sem("gates_ready")
        silu_spread = sem("silu_spread")
        held = {e: sem(f"held_{n}") for n, e in (("sp", nc.sync.engine), ("pool", nc.gpsimd.engine), ("dve", nc.vector.engine),
                                                 ("pe", nc.tensor.engine))}

        BEFORE = ["wT", "c", "mod", "ln1_0", "q_0", "k_0", "v_0", "ln1_1", "q_1", "k_1", "m0", "shared1", "shared2"]
        AT_SLOT = [["m1", "v"], ["y3"], ["yT"], ["out"], ["m2"], ["y0"], ["ln1"], ["h2T"], ["m3"], ["y1"], ["lg"], ["q"],
                   ["m0"], ["y2"], ["k"], ["rank"]]
        STEADY = [u for slot in AT_SLOT for u in slot]
        OF_BEFORE = ("y3", "yT", "out", "h2T", "lg", "rank")
        OF_AFTER = ("v", "ln1", "q", "k", "m0")
        FIRST = [u for u in STEADY if u not in OF_BEFORE]
        LAST = [u for u in STEADY if u not in OF_AFTER]
        LAST += [u + "_last" for u in OF_BEFORE]

        class Batch:

            def __init__(self, const, it=0):
                self.const, self.it = const, it
                self.n = 2 * it + const
                self.par = const % 2
                self.half = it + const // 2

            def plus(self, k):
                return Batch(self.const + k, self.it)

        def use(b, what):
            if b.const == -1:
                return BEFORE.index(what)
            if b.const == 0:
                return len(BEFORE) + FIRST.index(what)
            steady = len(BEFORE) + len(FIRST) + (b.n - 1) * len(STEADY)
            return steady + (LAST if b.const == B - 1 else STEADY).index(what)

        STACK_DMAS = 16 * (1 + PARTS)
        BATCH_ROWS = 16 * K_TOP * TT
        CHOOSE_STEPS = 2 + 2 * TT + 3 + 1
        AHEAD, B0, B1, B_LAST = Batch(-1), Batch(0), Batch(1), Batch(B - 1)

        def batches(eng, body):
            body(B0, True, False)
            with eng.Fori(0, (B - 2) // 2) as it:
                for k in (1, 2):
                    body(Batch(k, it), False, False)
            body(B_LAST, False, True)

        def group_ahead(b, g):
            return (b, g + 2) if g + 2 < G else (b.plus(1), g + 2 - G)

        def hold(eng, sem_, value):
            eng.wait_ge(sem_, value)
            eng.sem_inc(held[eng.engine], 1)

        block = ctx.enter_context(nc.Block())

        @block.sync
        def _(sp):
            for i, w in enumerate((Wq, Wk, Wv, Wp)):
                sp.dma_start(w_nat[:, i, :], w).then_inc(w_loaded, 16)
            sp.dma_start(x_in[:], x[0].rearrange("(t p) c -> p t c", p=P)).then_inc(x_in_loaded, 16)
            sp.dma_start(c_nat[:], c).then_inc(c_loaded, 16)
            for i, v in enumerate((bq, bk, bv)):
                sp.dma_start(bias_qkv[:, i:i + 1], v.rearrange("(p o) -> p o", o=1)).then_inc(small_loaded, 16)
            sp.dma_start(bp_bc[:], bp.partition_broadcast(P)).then_inc(small_loaded, 16)
            sp.dma_start(router_nat[:], router_w).then_inc(c_loaded, 16)
            sp.dma_start(router_bias[:], routing_bias.partition_broadcast(P)).then_inc(small_loaded, 16)
            sp.dma_start(nat[:, 0:2, :], sh_gate.rearrange("(j p) c -> p j c", p=P)).then_inc(shared_loaded, 16)
            sp.dma_start(nat[:, 2:4, :], sh_up.rearrange("(j p) c -> p j c", p=P)).then_inc(shared_loaded, 16)
            sp.dma_start(nat[:, 4:6, :], sh_down.rearrange("c (j i) -> c j i", j=IC)).then_inc(shared_loaded, 16)

            def load_x(b):
                sp.wait_ge(ln1_ready, TT * b.n)
                sp.dma_start(x_in[:], x[bass.ds(b.n % B, 1)].rearrange("o (t p) c -> p (o t) c", p=P)).then_inc(x_in_loaded, 16)

            def store_parts(b):
                for i, (parts, dram, stored) in enumerate(((qk_parts[0], q_dram, q_stored), (qk_parts[1], k_dram, k_stored))):
                    if b.const > 0:
                        before = b.plus(-1)
                        hold(sp, stack_loaded[before.par], STACK_DMAS * (before.half + 1))
                    sp.wait_ge(parts_ready, 2 * b.n + i + 1)
                    for j in range(PARTS):
                        sp.dma_start(dram[j].rearrange("d h t -> h d t"), parts[:, j, :]).then_inc(stored, 16)

            def load_stacks(b):
                if b.const >= 2:
                    sp.wait_ge(pv_done, SLOTS * (b.n - 1))
                else:
                    sp.wait_ge(stacks_cleared, 6)
                sp.wait_ge(q_stored, 48 * (b.n + 1))
                sp.wait_ge(k_stored, 48 * (b.n + 1))
                sp.dma_start(qs[b.par][0:PROD],
                             q_dram.rearrange("i d h t -> (i d) (h t)").unsqueeze(0).to_broadcast([PARTS, PARTS * DH, H * T])
                             ).then_inc(stack_loaded[b.par], 16)
                for j in range(PARTS):
                    r = j * PARTS * DH
                    sp.dma_start(ks[b.par][r:r + PARTS * DH],
                                 k_dram[j].rearrange("d h t -> d (h t)").unsqueeze(0).to_broadcast([PARTS, DH, H * T])
                                 ).then_inc(stack_loaded[b.par], 16)

            def load_x_again(b):
                if b.const > 0:
                    sp.wait_ge(stats2_ready, TT * b.n)
                sp.dma_start(x_ep[:], x[bass.ds(b.n, 1)].rearrange("o (t p) c -> p (o t) c", p=P)).then_inc(x_ep_loaded, 16)

            store_parts(B0)
            load_x(B1)
            load_stacks(B0)
            store_parts(B1)
            def body(b, first, last):
                if not last:
                    load_stacks(b.plus(1))
                load_x_again(b)
                if not last:
                    load_x(b.plus(2))
                    store_parts(b.plus(2))

            batches(sp, body)
            sp.wait_ge(pv_done, SLOTS * (B - 1))
            sp.dma_start(gate_up[:, :, 0:I], gate_w.rearrange("e c i -> c e i")).then_inc(routed_loaded, 16)
            sp.dma_start(gate_up[:, :, I:2 * I], up_w.rearrange("e c i -> c e i")).then_inc(routed_loaded, 16)
            for j in range(IC):
                sp.dma_start(down[:, :, j, :], down_w[:, j * P:(j + 1) * P, :].rearrange("e i c -> i e c")).then_inc(routed_loaded, 16)
            sp.wait_ge(pad_ready, 2)
            sp.dma_start(routed_dram[E * REGION:E * REGION + P, :], pad_row[:]).then_inc(padding_written, 16)
            sp.wait_ge(tables_ready, 1)
            for e in range(E):
                row = sp.value_load(end_row[0:1, e:e + 1], min_val=e * REGION, max_val=e * REGION + TOKENS)
                sp.dma_start(routed_dram[bass.ds(row, P), :], pad_row[:]).then_inc(padding_written, 16)
            sp.wait_ge(padding_written, 16 * (E + 1))
            sp.wait_ge(scattered, BATCH_ROWS * B)
            sp.wait_ge(tables_ready, 3)

            def load_unit(u, slot, wait):
                row = sp.value_load(unit_row[0:1, bass.ds(u, 1)], min_val=0, max_val=E * REGION)
                if wait:
                    sp.wait_ge(xu_read, u - RING + 1)
                    sp.wait_ge(xuT_full, u - RING + 1)
                sp.dma_start(xu[slot], routed_dram[bass.ds(row, P), :]).then_inc(xu_loaded[slot], 16)

            for u in range(RING):
                load_unit(u, u, False)
            with sp.Fori(1, UNITS // RING) as it:
                for slot in range(RING):
                    load_unit(RING * it + slot, slot, True)

            for slot in range(RING):
                sp.wait_ge(yu_sent[slot], 16 * UNITS // RING)
            result_v = result_dram.rearrange("(k b t p) c -> p k b t c", k=K_TOP, b=B, p=P)
            out_v = out.rearrange("b (t p) c -> p b t c", p=P)
            for b in range(B):
                for k in range(K_TOP):
                    sp.dma_start(results[b][k], result_v[:, k, b]).then_inc(results_loaded[b], 16)
            for b in range(B):
                sp.wait_ge(out_ready, b + 1)
                sp.dma_start(out_v[:, b], x1[:, TT * b:TT * (b + 1), :]).then_inc(out_stored, 16)
            sp.wait_ge(out_stored, 16 * B)

        @block.gpsimd
        def _(pool):
            pool.memset(ident[:], 0.0).then_inc(setup_pool, 1)
            pool.wait_ge(setup_pool, 1)
            pool.affine_select(out=ident[:], in_=ident[:], compare_op=ALU.not_equal, fill=1.0, base=0,
                               pattern=[[-1, P]], channel_multiplier=1).then_inc(consts_ready, 1)
            pool.wait_ge(consts_ready, 1)
            pool.tensor_copy(ident_bf[:], ident[:]).then_inc(consts_ready, 1)
            pool.memset(minus_half[:], -0.5).then_inc(setup_pool, 1)
            pool.memset(ones_bf[:], 1.0).then_inc(setup_pool, 1)
            pool.wait_ge(setup_pool, 3)
            pool.affine_select(out=before[:], in_=ones_bf[:], compare_op=ALU.is_gt, fill=0.0, base=0,
                               pattern=[[1, P]], channel_multiplier=-1).then_inc(consts_ready, 1)
            pool.memset(marks[:], 0.0).then_inc(consts_ready, 1)
            pool.sem_inc(rows_free, 2)
            pool.iota(expert_no[:], pattern=[[1, E]], base=0, channel_multiplier=0,
                      allow_small_or_imprecise_dtypes=True).then_inc(consts_ready, 1)
            pool.iota(next_row[0][:], pattern=[[REGION, E]], base=0, channel_multiplier=0,
                      allow_small_or_imprecise_dtypes=True).then_inc(consts_ready, 1)
            for k in range(RING):
                pool.memset(digit[:, k:k + 1], float(E ** k)).then_inc(consts_ready, 1)
            pool.memset(pad_row[:], 0.0).then_inc(pad_ready, 1)
            pool.wait_ge(pad_ready, 1)
            pool.memset(pad_row[:, C + 1:C + 2], float(FAR)).then_inc(pad_ready, 1)
            pool.iota(first_row[:], pattern=[[REGION, E]], base=0, channel_multiplier=0,
                      allow_small_or_imprecise_dtypes=True).then_inc(consts_ready, 1)
            pool.iota(unit_start[:], pattern=[[P, UNITS]], base=0, channel_multiplier=0,
                      allow_small_or_imprecise_dtypes=True).then_inc(consts_ready, 1)
            pool.affine_select(out=earlier[:], in_=ones_bf[:, 0:E * E].rearrange("p (e f) -> p e f", e=E), compare_op=ALU.is_gt,
                               fill=0.0, base=0, pattern=[[1, E], [-1, E]], channel_multiplier=0).then_inc(consts_ready, 1)
            pool.iota(home[:], pattern=[[TOKENS, K_TOP], [P, TT]], base=0, channel_multiplier=1,
                      allow_small_or_imprecise_dtypes=True).then_inc(setup_pool, 1)
            for i in range(2):
                pool.memset(qs[i][:].rearrange("p h t -> p (h t)").bitcast(F32), 0.0).then_inc(stacks_cleared, 1)

            def rstd(mv, ve, ve_ready, out_, ready, stats_ready, b):
                hold(pool, stats_ready, TT * (b.n + 1))
                pool.tensor_scalar(ve[:], mv[:, :, 1], EPS, None, ALU.add).then_inc(ve_ready, 1)
                pool.wait_ge(ve_ready, b.n + 1)
                pool.tensor_tensor(out_[:], ve[:], minus_half[:], ALU.pow).then_inc(ready, 1)

            def split_qk(b, i, done):
                parts, f = qk_parts[i], qk_f[i]
                pool.wait_ge(misc_free, done + 1)
                if b.const > 0 or i > 0:
                    pool.wait_ge(parts_ready, 2 * b.n + i)
                pool.tensor_tensor(qk_r[:], f[:], parts[:, 0, :], ALU.subtract).then_inc(rest_ready, 1)
                hold(pool, rest_ready, 4 * b.n + 2 * i + 1)
                pool.tensor_copy(parts[:, 1, :], qk_r[:]).then_inc(rest_ready, 1)
                pool.wait_ge(rest_ready, 4 * b.n + 2 * i + 2)
                pool.tensor_tensor(parts[:, 2, :], qk_r[:], parts[:, 1, :], ALU.subtract).then_inc(parts_ready, 1)

            def residual(b):
                ga = ga_bc[:, bass.ds(b.n, 1), :].rearrange("p o c -> p (o c)")
                pool.tensor_tensor(bp_ga[:], bp_bc[:], ga, ALU.mult).then_inc(bp_ga_ready, 1)
                pool.tensor_tensor(wp_ga[:], wT[:, 3, :], ga, ALU.mult).then_inc(wp_ga_ready, 1)
                pool.wait_ge(bp_ga_ready, b.n + 1)
                pool.wait_ge(x_ep_loaded, 16 * (b.n + 1))
                pool.tensor_tensor(x_ep[:], x_ep[:], bp_ga[:].unsqueeze(1).to_broadcast([P, TT, C]),
                                   ALU.add).then_inc(xres_ready, 1)

            def modulate2(b):
                pool.wait_ge(ln2_ready, TT * (b.n + 1))
                pool.tensor_tensor(ln2[:], ln2[:], cb_bc[:, bass.ds(b.n, 1), :].to_broadcast([P, TT, C]),
                                   ALU.mult).then_inc(h2_chain, 1)
                pool.wait_ge(h2_chain, b.n + 1)
                pool.wait_ge(rows_free, b.n + 1)
                for k in range(K_TOP):
                    pool.tensor_tensor(rec[b.par][:, k, :, 0:C], ln2[:],
                                       sb_bc[:, bass.ds(b.n, 1), :].to_broadcast([P, TT, C]), ALU.add).then_inc(h2_ready, 1)
                pool.tensor_copy(rec[b.par][:, :, :, C + 1], home[:]).then_inc(home_ready, 1)
                hold(pool, home_ready, 2 * b.n + 1)
                pool.tensor_scalar(home[:], home[:], float(T), None, ALU.add).then_inc(home_ready, 1)

            def scatter(b):
                hold(pool, rows_ready, b.n + 1)
                for k in range(K_TOP):
                    for t in range(TT):
                        pool.indirect_dma_start(out=routed_dram, out_offset=bass.IndirectOffsetOnAxis(ap=row_u[:, k, t:t + 1], axis=0),
                                                in_=rec[b.par][:, k, t, :], in_offset=None).then_inc(scattered, 16)
                pool.wait_ge(scattered, BATCH_ROWS * (b.n + 1))
                pool.sem_inc(rows_free, 1)

            pool.wait_ge(setup_pool, 4)
            rstd(mv1, ve1, var1_ready, rstd1, rstd1_ready, stats1_ready, B0)
            pool.wait_ge(misc_free, use(AHEAD, "c") + 1)
            pool.tensor_copy(silu_bc, silu_T[:].unsqueeze(2).to_broadcast([P, B, P])).then_inc(silu_spread, 1)
            for i, w in enumerate("qk"):
                split_qk(B0, i, use(AHEAD, w + "_0"))
            rstd(mv1, ve1, var1_ready, rstd1, rstd1_ready, stats1_ready, B1)
            for i, w in enumerate("qk"):
                split_qk(B1, i, use(AHEAD, w + "_1"))

            def body(b, first, last):
                if not first:
                    rstd(mv2, ve2, var2_ready, rstd2, rstd2_ready, stats2_ready, b.plus(-1))
                if not last:
                    rstd(mv1, ve1, var1_ready, rstd1, rstd1_ready, stats1_ready, b.plus(2))
                if not first:
                    modulate2(b.plus(-1))
                residual(b)
                if not last:
                    split_qk(b.plus(2), 0, use(b, "q"))
                    split_qk(b.plus(2), 1, use(b, "k"))
                if not first:
                    scatter(b.plus(-1))

            pool.wait_ge(gates_ready, 2)
            batches(pool, body)
            rstd(mv2, ve2, var2_ready, rstd2, rstd2_ready, stats2_ready, B_LAST)
            modulate2(B_LAST)
            scatter(B_LAST)

            def send_unit(u, slot):
                hold(pool, yu_ready, u + 1)
                pool.indirect_dma_start(out=result_dram, out_offset=bass.IndirectOffsetOnAxis(ap=home_u[:, slot:slot + 1], axis=0),
                                        in_=y_u[slot], in_offset=None, bounds_check=K_TOP * TOKENS - 1,
                                        oob_is_err=False).then_inc(yu_sent[slot], 16)

            with pool.Fori(0, UNITS // RING) as it:
                for slot in range(RING):
                    send_unit(RING * it + slot, slot)
            for b in range(B):
                r = results[b]
                pool.wait_ge(results_loaded[b], 16 * K_TOP)
                pool.tensor_tensor(r[0], r[0], r[1], ALU.add).then_inc(results_added, 1)

        @block.scalar
        def _(act):
            act.dma_start(wmod_sb[:], wmod).then_inc(c_loaded, 16)
            act.wait_ge(misc_full, use(AHEAD, "wT") + 1)
            act.activation(wT[:].rearrange("p i c -> p (i c)"), misc[:], ACT.Copy).then_inc(misc_free, 1)
            act.wait_ge(misc_full, use(AHEAD, "c") + 1)
            act.activation(router_T[:], misc[:, B:B + E], ACT.Copy)
            act.activation(silu_T[:], misc[:, 0:B], ACT.Silu).then_inc(misc_free, 1)
            act.wait_ge(misc_full, use(AHEAD, "mod") + 1)
            act.activation(mod_T[:, 0, :], misc[:, 0:B], ACT.Identity)
            act.activation(mod_T[:, 1, :], misc[:, B:2 * B], ACT.Identity, bias=1.0).then_inc(misc_free, 1)
            act.wait_ge(misc_free, use(AHEAD, "mod") + 1)
            act.wait_ge(small_loaded, 80)

            def project_in(b, done):
                act.wait_ge(misc_full, done + 1)
                nb = b.n % B
                act.activation(hT[:], misc[:], ACT.Identity, bias=mod_T[:, 0, bass.ds(nb, 1)],
                               scale=mod_T[:, 1, bass.ds(nb, 1)]).then_inc(misc_free, 1)

            def evacuate_qk(b, i, done):
                act.wait_ge(misc_full, done + 1)
                if b.const > 0:
                    act.wait_ge(parts_ready, 2 * (b.n - 1) + i + 1)
                    act.wait_ge((q_stored, k_stored)[i], 48 * b.n)
                act.activation(qk_parts[i][:, 0, :], misc[:], ACT.Identity, bias=bias_qkv[:, i:i + 1])
                act.activation(qk_f[i][:], misc[:], ACT.Identity, bias=bias_qkv[:, i:i + 1]).then_inc(misc_free, 1)

            def evacuate_v(b, done):
                act.wait_ge(misc_full, done + 1)
                act.activation(vs[b.par][:, :, :, 0:DH], misc[:].rearrange("p (t h d) -> p t h d", t=TT, d=DH),
                               ACT.Copy).then_inc(misc_free, 1)

            def max_rows(b, g, done):
                grp = G * b.n + g
                act.wait_ge(misc_full, done + 1)
                if b.const > 0 or g >= 2:
                    act.wait_ge(m_row_loaded[g % 2], 16 * (2 * b.n + g // 2))
                act.activation(m_rows[g % 2][:], misc_bf[0:PARTS * HG * TT, 0:P], ACT.Copy).then_inc(misc_free, 1)
                act.wait_ge(misc_free, done + 1)
                act.dma_start(qs[b.par][MROW:MROW + PARTS, HG * g:HG * (g + 1), :].rearrange("p h (t q) -> p (h t) q", t=TT),
                              m_rows[g % 2][:]).then_inc(m_row_loaded[g % 2], 16)

            def exponentials(b, n):
                quad = SLOTS * b.n + n
                if b.const > 0 or n >= 2:
                    act.wait_ge(pv_done, quad - 1)
                for hh in range(HG):
                    act.wait_ge(st_full, HG * quad + hh + 1)
                    act.activation(pt[n % 2][:, hh, :], st_bank[hh % 2][:], ACT.Exp, scale=SCALE).then_inc(exp_done, 1)

            def evacuate_y(b, g):
                act.wait_ge(pv_done, SLOTS * b.n + TT * (g + 1))
                act.activation(y_strips[:], pv_bank[:], ACT.Copy).then_inc(y_evacuated, 1)

            def evacuate_yT(done):
                act.wait_ge(misc_full, done + 1)
                act.activation(yT[:], misc[:], ACT.Identity, bias=bias_qkv[:, 2:3]).then_inc(misc_free, 1)

            def evacuate_h2T(b, done):
                act.wait_ge(misc_full, done + 1)
                act.activation(h2T_now[:], misc[:], ACT.Copy)
                act.activation(h2T[:, bass.ds(T * b.n, T)], misc[:], ACT.Copy).then_inc(misc_free, 1)

            def exp_minus_logits(b, done):
                act.wait_ge(misc_free, done + 1)
                act.activation(probs[:], logits[:], ACT.Exp, scale=-1.0).then_inc(sig_exp, 1)

            project_in(B0, use(AHEAD, "ln1_0"))
            for i, w in enumerate("qk"):
                evacuate_qk(B0, i, use(AHEAD, w + "_0"))
            act.wait_ge(stacks_cleared, 6)
            evacuate_v(B0, use(AHEAD, "v_0"))
            project_in(B1, use(AHEAD, "ln1_1"))
            for i, w in enumerate("qk"):
                evacuate_qk(B1, i, use(AHEAD, w + "_1"))
            max_rows(B0, 0, use(AHEAD, "m0"))
            act.wait_ge(misc_full, use(AHEAD, "shared1") + 1)
            act.activation(shared_w[:].rearrange("p j i -> p (j i)"), misc[:], ACT.Copy).then_inc(misc_free, 1)
            act.wait_ge(misc_full, use(AHEAD, "shared2") + 1)
            act.activation(shared_down[:].rearrange("p j c -> p (j c)"), misc[:, 0:IC * C], ACT.Copy).then_inc(misc_free, 1)

            def body(b, first, last):
                for n in range(SLOTS):
                    exponentials(b, n)
                    if n == 0:
                        if not first:
                            evacuate_y(b.plus(-1), G - 1)
                        max_rows(b, 1, use(b, "m1"))
                        if not last:
                            evacuate_v(b.plus(1), use(b, "v"))
                    if n in (4, 8, 12):
                        evacuate_y(b, n // 4 - 1)
                    if n == 2 and not first:
                        evacuate_yT(use(b, "yT"))
                    if n in (4, 8):
                        max_rows(b, n // 4 + 1, use(b, f"m{n // 4 + 1}"))
                    if n == 6 and not last:
                        project_in(b.plus(2), use(b, "ln1"))
                    if n == 7 and not first:
                        evacuate_h2T(b.plus(-1), use(b, "h2T"))
                    if n == 10 and not first:
                        exp_minus_logits(b.plus(-1), use(b, "lg"))
                    if n == 11 and not last:
                        evacuate_qk(b.plus(2), 0, use(b, "q"))
                    if n == 12 and not last:
                        max_rows(b.plus(1), 0, use(b, "m0"))
                    if n == 14 and not last:
                        evacuate_qk(b.plus(2), 1, use(b, "k"))

            batches(act, body)
            def shared_silu(b):
                for j in range(IC):
                    act.wait_ge(s_full, IC * b + j + 1)
                    if b >= 1:
                        act.wait_ge(s_act, IC * (b - 1) + j + 1)
                    act.activation(silu_s[:, j, :], mx_bank[j][:, 0, :], ACT.Silu).then_inc(s_silu, 1)

            evacuate_y(B_LAST, G - 1)
            shared_silu(0)
            shared_silu(1)
            evacuate_yT(use(B_LAST, "yT_last"))
            shared_silu(2)
            shared_silu(3)
            shared_silu(4)
            evacuate_h2T(B_LAST, use(B_LAST, "h2T_last"))
            exp_minus_logits(B_LAST, use(B_LAST, "lg_last"))
            shared_silu(5)
            shared_silu(6)
            shared_silu(7)

            def unit_xT(u, slot):
                act.wait_ge(xuT_full, u + 1)
                act.activation(xuT[slot % 2], mx_bank[0][:, slot % 2, 0:P], ACT.Copy).then_inc(xuT_ready, 1)

            def unit_silu(u, slot, wait):
                act.wait_ge(gu_full, u + 1)
                if wait:
                    act.wait_ge(act_ready, u - 1)
                act.activation(silu_u[slot % 2], st_bank[slot % 2][:, 0:I], ACT.Silu).then_inc(silu_ready, 1)

            def unit_y(u, slot, turn, wait):
                act.wait_ge(yu_full, u + 1)
                if wait:
                    act.wait_ge(yu_sent[slot], 16 * turn)
                act.activation(y_u[slot], (pv_bank, misc)[slot % 2][:, 0:C], ACT.Copy, scale=w_u[slot]).then_inc(yu_ready, 1)

            def unit_step(i, k, turn, has_silu=True, has_xT=True, has_y=True, wait_silu=True, wait_y=True):
                if has_silu:
                    unit_silu(i, k % RING, wait_silu)
                if has_xT:
                    unit_xT(i + 1, (k + 1) % RING)
                if has_y:
                    unit_y(i - 2, (k - 2) % RING, turn + (k - 2) // RING, wait_y)

            unit_xT(0, 0)
            for i in range(RING + 2):
                unit_step(i, i % RING, i // RING, has_y=i >= 2, wait_silu=i >= 2, wait_y=False)
            for i in range(RING + 2, 2 * RING):
                unit_step(i, i % RING, i // RING)
            with act.Fori(2, UNITS // RING - 1) as it:
                for k in range(RING):
                    unit_step(RING * it + k, k, it)
            for i in range(UNITS - RING, UNITS + 2):
                unit_step(i, i % RING, i // RING, has_silu=i < UNITS, has_xT=i + 1 < UNITS)

        @block.vector
        def _(dve):
            two_ones = 1.0 + 0x3F80 * 2.0 ** -23
            dve.wait_ge(w_loaded, 64)
            dve.tensor_reduce(alpha[:], w_nat[:], AX_X, ALU.add, apply_absolute_value=True).then_inc(setup_dve, 1)
            dve.tensor_scalar(w_sgn, w_nat[:], 0.0, None, ALU.is_gt)
            dve.tensor_scalar(w_neg, w_nat[:], 0.0, None, ALU.is_lt).then_inc(setup_dve, 1)
            dve.wait_ge(setup_dve, 2)
            dve.tensor_tensor(w_sgn, w_sgn, w_neg, ALU.subtract).then_inc(setup_dve, 1)
            dve.wait_ge(setup_dve, 3)
            for i in range(4):
                dve.tensor_scalar(w_nat[:, i, :], w_sgn[:, i, :], alpha[:, i:i + 1], 1.0 / C, ALU.mult,
                                  ALU.mult).then_inc(setup_dve, 1)

            def stats(src, st, mv, chain, ready, b):
                for t in range(TT):
                    dve.bn_stats(st[:, t, :], src(t)).then_inc(chain, 1)
                for t in range(TT):
                    hold(dve, chain, TT * b.n + t + 1)
                    dve.bn_aggr(mv[:, t, :], st[:, t, :]).then_inc(ready, 1)

            def normalise(src, mv, rstd_, rstd_ready, dst, ready, b):
                dve.wait_ge(rstd_ready, b.n + 1)
                for t in range(TT):
                    dve.tensor_scalar(dst[:, t, :], src(t), mv[:, t, 0:1], rstd_[:, t:t + 1], ALU.subtract,
                                      ALU.mult).then_inc(ready, 1)

            def stats1(b):
                dve.wait_ge(x_in_loaded, 16 * (b.n + 1))
                stats(lambda t: x_in[:, t, :], stats1_sb, mv1, stats1_chain, stats1_ready, b)

            def layer_norm1(b):
                normalise(lambda t: x_in[:, t, :], mv1, rstd1, rstd1_ready, ln1, ln1_ready, b)

            def x1_tile(b):
                return lambda t: x1[:, bass.ds(TT * b.n + t, 1), :].rearrange("p o c -> p (o c)")

            def stats2(b):
                stats(x1_tile(b), stats2_sb, mv2, stats2_chain, stats2_ready, b)

            def layer_norm2(b):
                normalise(x1_tile(b), mv2, rstd2, rstd2_ready, ln2, ln2_ready, b)

            def maxima(b, g, hh):
                for half in range(2):
                    fill = 2 * HG * (G * b.n + g) + 2 * hh + half
                    dve.wait_ge(mx_full, fill + 1)
                    dve.tensor_reduce(neg_max[g % 2][:, hh, 2 * half:2 * half + 2], mx_bank[half][:], AX_X, ALU.max,
                                      negate=True).then_inc(mx_free, 1)

            def split_max(b, g):
                grp = G * b.n + g
                nm = neg_max[g % 2][:].rearrange("p h t -> p (h t)")
                dve.wait_ge(mx_free, 2 * HG * (grp + 1))
                if b.const > 0 or g > 0:
                    dve.wait_ge(m_split, grp)
                    dve.wait_ge(m_row_loaded[(g - 1) % 2], 16 * (2 * b.n + (g - 1) // 2 + 1))
                dve.tensor_copy(m_parts[:, 0, :], nm).then_inc(m_chain, 1)
                dve.wait_ge(m_chain, 3 * grp + 1)
                dve.tensor_tensor(m_rest[:], nm, m_parts[:, 0, :], ALU.subtract).then_inc(m_chain, 1)
                dve.wait_ge(m_chain, 3 * grp + 2)
                dve.tensor_copy(m_parts[:, 1, :], m_rest[:]).then_inc(m_chain, 1)
                dve.wait_ge(m_chain, 3 * grp + 3)
                dve.tensor_tensor(m_parts[:, 2, :], m_rest[:], m_parts[:, 1, :], ALU.subtract).then_inc(m_split, 1)

            def normalise_y(b, g, done):
                y = misc[:].rearrange("p (t s d) -> p t s d", t=TT, d=32)
                dve.wait_ge(misc_full, done + 1)
                dve.reciprocal(y_rden[:], y[:, :, :, DH]).then_inc(rden_ready, 1)
                dve.wait_ge(rden_ready, G * b.n + g + 1)
                dve.tensor_tensor(y_tok[:, :, g * 32:(g + 1) * 32].rearrange("p t (s d) -> p t s d", d=DH),
                                  y[:, :, :, 0:DH], y_rden[:].unsqueeze(3).to_broadcast([P, TT, HG, DH]),
                                  ALU.mult).then_inc(misc_free, 1)

            def residual_sum(b, done):
                dve.wait_ge(xres_ready, b.n + 1)
                dve.wait_ge(misc_full, done + 1)
                dve.tensor_tensor(x1[:, bass.ds(TT * b.n, TT), :], misc[:].rearrange("p (t c) -> p t c", t=TT), x_ep[:],
                                  ALU.add).then_inc(misc_free, 1)
                hold(dve, misc_free, done + 1)

            def add_router_bias(b, done):
                dve.wait_ge(misc_full, done + 1)
                dve.tensor_tensor(logits[:], misc[:, 0:TT * E].rearrange("p (t e) -> p t e", t=TT),
                                  router_bias[:].unsqueeze(1).to_broadcast([P, TT, E]), ALU.add).then_inc(misc_free, 1)

            def choose(b):
                count = [0]

                def link(ins, wait=True):
                    count[0] += 1
                    ins.then_inc(route_chain, 1)
                    if wait:
                        hold(dve, route_chain, CHOOSE_STEPS * b.n + count[0])

                dve.wait_ge(sig_exp, b.n + 1)
                link(dve.tensor_scalar(probs[:], probs[:], 1.0, None, ALU.add))
                link(dve.reciprocal(probs[:], probs[:]))
                for t in range(TT):
                    link(dve.max(top_p[:, t, :], probs[:, t, :]), wait=t == TT - 1)
                for t in range(TT):
                    link(dve.max_index(top_e[:, t, :], top_p[:, t, :], probs[:, t, :]), wait=t == TT - 1)
                link(dve.tensor_copy(top_ef[:], top_e[:, :, 0:K_TOP]), wait=False)
                link(dve.tensor_tensor(p_sum[:], top_p[:, :, 0], top_p[:, :, 1], ALU.add))
                link(dve.reciprocal(p_rsum[:], p_sum[:]))
                dve.wait_ge(rows_free, b.n + 1)
                for k in range(K_TOP):
                    dve.tensor_tensor(rec[b.par][:, k, :, C], top_p[:, :, k], p_rsum[:], ALU.mult).then_inc(weights_ready, 1)
                link(dve.tensor_tensor(chosen[:], expert_no[:].unsqueeze(1).unsqueeze(1).to_broadcast([P, K_TOP, TT, E]),
                                       top_ef[:].rearrange("p t k -> p k t").unsqueeze(3).to_broadcast([P, K_TOP, TT, E]),
                                       ALU.is_equal))
                assert count[0] == CHOOSE_STEPS
                dve.tensor_tensor(marks[:, 0:TT, :], chosen[:, 0], chosen[:, 1], ALU.add).then_inc(marks_ready, 1)

            def assign_rows(b, done):
                now, nxt = next_row[b.par], next_row[1 - b.par]
                dve.wait_ge(misc_full, done + 1)
                dve.tensor_tensor(place[:], misc[:, 0:TT * E].rearrange("p (t e) -> p t e", t=TT),
                                  now[:].unsqueeze(1).to_broadcast([P, TT, E]), ALU.add).then_inc(rank_chain, 1)
                dve.tensor_tensor(nxt[:], now[:], misc[:, TT * E:(TT + 1) * E], ALU.add).then_inc(misc_free, 1)
                dve.wait_ge(rank_chain, 3 * b.n + 1)
                dve.tensor_tensor(picked[:], chosen[:], place[:].unsqueeze(1).to_broadcast([P, K_TOP, TT, E]),
                                  ALU.mult).then_inc(rank_chain, 1)
                dve.wait_ge(rank_chain, 3 * b.n + 2)
                dve.tensor_reduce(row_f[:], picked[:], AX_X, ALU.add).then_inc(rank_chain, 1)
                dve.wait_ge(rank_chain, 3 * b.n + 3)
                dve.wait_ge(rows_free, b.n + 2)
                dve.tensor_copy(row_u[:], row_f[:]).then_inc(rows_ready, 1)

            stats1(B0)
            for i in range(2):
                dve.memset(ks[i][:].rearrange("p h t -> p (h t)").bitcast(F32), 0.0).then_inc(setup_dve, 1)
                dve.wait_ge(setup_dve, 8 + i)
                dve.memset(ks[i][MROW:MROW + PARTS].rearrange("p h t -> p (h t)").bitcast(F32),
                           two_ones).then_inc(stacks_cleared, 1)
                if i == 0:
                    layer_norm1(B0)
                dve.memset(vs[i][:], 0.0).then_inc(v_cleared, 1)
                dve.wait_ge(v_cleared, i + 1)
                dve.memset(vs[i][:, :, :, DH], 1.0).then_inc(stacks_cleared, 1)
            stats1(B1)
            layer_norm1(B1)
            kinds = (ga_bc, sb_bc, cb_bc, gb_bc)
            for b in range(B):
                dve.wait_ge(bc_full, b + 1)
                bank = mx_bank[(b // 2) % 2][:, b % 2, :]
                for k, dst in enumerate(kinds):
                    dve.tensor_scalar(dst[:, b, :], bank[:, k * C:(k + 1) * C], 1.0 if dst is cb_bc else 0.0, None,
                                      ALU.add).then_inc(bc_free, 1)
            dve.wait_ge(bc_free, 4 * B)
            for k, g_bc in enumerate((ga_bc, gb_bc)):
                dve.tensor_scalar(gate_sign, g_bc[:], 0.0, 2.0, ALU.is_ge, ALU.mult).then_inc(gate_chain, 1)
                dve.wait_ge(gate_chain, 3 * k + 1)
                dve.scalar_tensor_tensor(g_bc[:], g_bc[:], -1.0, g_bc[:], ALU.mult, ALU.max).then_inc(gate_chain, 1)
                dve.wait_ge(gate_chain, 3 * k + 2)
                dve.tensor_scalar(g_bc[:], g_bc[:], 0.25, None, ALU.max).then_inc(gate_chain, 1)
                dve.wait_ge(gate_chain, 3 * k + 3)
                dve.scalar_tensor_tensor(g_bc[:], gate_sign, -1.0, g_bc[:], ALU.add, ALU.mult).then_inc(gates_ready, 1)
                dve.wait_ge(gates_ready, k + 1)

            for g in range(2):
                for hh in range(HG):
                    maxima(B0, g, hh)
                split_max(B0, g)

            def body(b, first, last):
                for n in range(SLOTS):
                    if n < 8 or not last:
                        maxima(*group_ahead(b, n // TT), n % TT)
                        if n % TT == TT - 1:
                            split_max(*group_ahead(b, n // TT))
                    if n == 1 and not first:
                        normalise_y(b.plus(-1), G - 1, use(b, "y3"))
                    if n in (5, 9, 13):
                        normalise_y(b, n // 4 - 1, use(b, f"y{n // 4 - 1}"))
                    if n == 3 and not first:
                        residual_sum(b.plus(-1), use(b, "out"))
                        stats2(b.plus(-1))
                    if n == 4 and not last:
                        stats1(b.plus(2))
                    if n == 5 and not first:
                        layer_norm2(b.plus(-1))
                    if n == 5 and not last:
                        layer_norm1(b.plus(2))
                    if n == 10 and not first:
                        add_router_bias(b.plus(-1), use(b, "lg"))
                    if n == 11 and not first:
                        choose(b.plus(-1))
                    if n == 15 and not first:
                        assign_rows(b.plus(-1), use(b, "rank"))

            batches(dve, body)
            def shared_act(b):
                for j in range(IC):
                    dve.wait_ge(s_silu, IC * b + j + 1)
                    if b >= 2:
                        dve.wait_ge(s_down, b - 1)
                    dve.tensor_tensor(act_s[:, b % 2, j, :], silu_s[:, j, :], mx_bank[j][:, 1, :], ALU.mult).then_inc(s_act, 1)

            def shared_sum(b):
                dve.wait_ge(s_down, b + 1)
                if b >= 1:
                    dve.wait_ge(s_out, b)
                dve.tensor_tensor(gated, st_bank[b % 2][:].rearrange("p (t c) -> p t c", t=TT),
                                  gb_bc[:, b:b + 1, :].to_broadcast([P, TT, C]), ALU.mult).then_inc(s_gated, 1)
                dve.wait_ge(s_gated, b + 1)
                dve.tensor_tensor(x1[:, TT * b:TT * (b + 1), :], x1[:, TT * b:TT * (b + 1), :], gated, ALU.add).then_inc(s_out, 1)

            def tables():
                count = [0]

                def link(ins):
                    count[0] += 1
                    ins.then_inc(table_chain, 1)
                    dve.wait_ge(table_chain, count[0])

                used = next_row[B % 2]
                dve.wait_ge(misc_free, use(B_LAST, "rank_last") + 1)
                dve.tensor_copy(end_row[:], used[:]).then_inc(tables_ready, 1)
                link(dve.tensor_tensor(padded[:], used[:], first_row[:], ALU.subtract))
                link(dve.tensor_scalar(padded_i[:], padded[:], float(P - 1), None, ALU.add))
                shift = P.bit_length() - 1
                link(dve.tensor_scalar(padded_i[:], padded_i[:], shift, shift, ALU.logical_shift_right, ALU.logical_shift_left))
                link(dve.tensor_copy(padded[:], padded_i[:]))
                link(dve.tensor_tensor(entered[:, 0:E, :], earlier[:], padded[:].unsqueeze(1).to_broadcast([P, E, E]), ALU.mult))
                link(dve.tensor_reduce(region_end[:], entered[:, 0:E, :], AX_X, ALU.add))
                link(dve.tensor_tensor(region_end[:], region_end[:], padded[:], ALU.add))
                link(dve.tensor_scalar(skip[:], padded[:], -1.0, float(REGION), ALU.mult, ALU.add))
                link(dve.memset(skip[:, E - 1:E], float(FAR)))
                link(dve.tensor_tensor(entered[:], unit_start[:].unsqueeze(2).to_broadcast([P, UNITS, E]),
                                       region_end[:].unsqueeze(1).to_broadcast([P, UNITS, E]), ALU.is_ge))
                link(dve.tensor_tensor(skipped[:], entered[:], skip[:].unsqueeze(1).to_broadcast([P, UNITS, E]), ALU.mult))
                link(dve.tensor_reduce(unit_f[:, 0, :], skipped[:], AX_X, ALU.add))
                link(dve.tensor_reduce(unit_f[:, 1, :], entered[:, :, 0:E - 1], AX_X, ALU.add))
                link(dve.tensor_tensor(unit_f[:, 0, :], unit_f[:, 0, :], unit_start[:], ALU.add))
                dve.tensor_scalar(unit_row[:], unit_f[:, 0, :], float(E * REGION), None, ALU.min).then_inc(tables_ready, 1)
                link(dve.tensor_tensor(digits[:], unit_f[:, 1, :].rearrange("p (g k) -> p g k", k=RING),
                                       digit[:].unsqueeze(1).to_broadcast([P, UNITS // RING, RING]), ALU.mult))
                link(dve.tensor_reduce(packed_f[:], digits[:], AX_X, ALU.add))
                dve.tensor_copy(turn_experts[:], packed_f[:]).then_inc(tables_ready, 1)

            shared_act(0)
            normalise_y(B_LAST, G - 1, use(B_LAST, "y3_last"))
            shared_act(1)
            shared_sum(0)
            shared_act(2)
            shared_sum(1)
            residual_sum(B_LAST, use(B_LAST, "out_last"))
            stats2(B_LAST)
            shared_act(3)
            shared_sum(2)
            layer_norm2(B_LAST)
            shared_act(4)
            shared_sum(3)
            add_router_bias(B_LAST, use(B_LAST, "lg_last"))
            shared_act(5)
            choose(B_LAST)
            shared_sum(4)
            shared_act(6)
            shared_sum(5)
            assign_rows(B_LAST, use(B_LAST, "rank_last"))
            tables()
            shared_act(7)
            shared_sum(6)
            shared_sum(7)

            def unit_rows(u, slot, turn, wait):
                dve.wait_ge(xu_loaded[slot], 16 * (turn + 1))
                if wait:
                    dve.wait_ge(yu_sent[slot], 16 * turn)
                dve.tensor_copy(w_u[slot], xu[slot][:, C:C + 1])
                dve.tensor_copy(home_u[:, slot:slot + 1], xu[slot][:, C + 1:C + 2]).then_inc(xu_read, 1)

            def unit_act(u, slot, wait):
                dve.wait_ge(silu_ready, u + 1)
                if wait:
                    dve.wait_ge(actT_full, u - 1)
                dve.tensor_tensor(act_u[slot % 2], silu_u[slot % 2], st_bank[slot % 2][:, I:2 * I], ALU.mult).then_inc(act_ready, 1)

            def unit_actT(u, slot, wait):
                dve.wait_ge(actT_full, u + 1)
                if wait:
                    dve.wait_ge(yu_full, u - 1)
                dve.tensor_copy(actT_u[slot % 2], mx_bank[1][:, slot % 2, 0:I]).then_inc(actT_ready, 1)

            def unit_step(i, k, turn, has_rows=True, has_actT=True, has_act=True, first=False, reuse=True):
                if has_actT:
                    unit_actT(i - 1, (k - 1) % RING, not first)
                if has_act:
                    unit_act(i, k % RING, not first)
                if has_rows:
                    unit_rows(i + 2, (k + 2) % RING, turn + (k + 2) // RING, reuse)

            unit_rows(0, 0, 0, False)
            unit_rows(1, 1, 0, False)
            for i in range(RING):
                unit_step(i, i, 0, has_actT=i > 0, first=i < 2, reuse=i + 2 >= RING)
            with dve.Fori(1, UNITS // RING - 1) as it:
                for k in range(RING):
                    unit_step(RING * it + k, k, it)
            for i in range(UNITS - RING, UNITS + 1):
                unit_step(i, i % RING, i // RING, has_rows=i + 2 < UNITS, has_act=i < UNITS)
            for b in range(B):
                r = results[b][0]
                xb = x1[:, TT * b:TT * (b + 1), :]
                dve.wait_ge(results_added, b + 1)
                dve.tensor_tensor(r, r, gb_bc[:, b:b + 1, :].to_broadcast([P, TT, C]), ALU.mult).then_inc(out_chain, 1)
                dve.wait_ge(out_chain, b + 1)
                dve.tensor_tensor(xb, xb, r, ALU.add).then_inc(out_ready, 1)

        @block.tensor
        def _(pe):
            def transposes(src):
                for t in range(TT):
                    last = pe.transpose(misc[:, t * P:(t + 1) * P], src(t), ident[:])
                return last

            def free(done):
                pe.wait_ge(misc_free, done)

            pe.wait_ge(consts_ready, 2)
            pe.wait_ge(setup_dve, 7)
            transposes(lambda i: w_nat[:, i, :]).then_inc(misc_full, 1)
            free(use(AHEAD, "c"))
            pe.wait_ge(c_loaded, 48)
            pe.transpose(misc[:, 0:B], c_nat[:], ident[0:B, 0:B])
            pe.transpose(misc[:, B:B + E], router_nat[:], ident[0:E, 0:E]).then_inc(misc_full, 1)
            free(use(AHEAD, "mod"))
            for j in range(2):
                last = pe.matmul(misc[:, j * B:(j + 1) * B], wmod_sb[:, j * C:(j + 1) * C], silu_T[:],
                                 start=True, stop=True)
            last.then_inc(misc_full, 1)

            def ln1_T(b, done):
                free(done)
                pe.wait_ge(ln1_ready, TT * (b.n + 1))
                transposes(lambda t: ln1[:, t, :]).then_inc(misc_full, 1)

            def project(i, done):
                free(done)
                pe.matmul(misc[:], wT[:, i, :], hT[:], start=True, stop=True).then_inc(misc_full, 1)

            def project_v(done):
                free(done)
                for t in range(TT):
                    last = pe.matmul(misc[:, t * P:(t + 1) * P], hT[:, t * P:(t + 1) * P], wT[:, 2, :],
                                     start=True, stop=True)
                last.then_inc(misc_full, 1)

            def max_T(b, g, done):
                free(done)
                hold(pe, m_split, G * b.n + g + 1)
                pe.transpose(misc_bf[0:PARTS * HG * TT, 0:P], m_parts[:].rearrange("p j m -> p (j m)"),
                             ident_bf[:]).then_inc(misc_full, 1)

            def y_T(b, g, done):
                free(done)
                pe.wait_ge(y_evacuated, G * b.n + g + 1)
                transposes(lambda t: y_strips[:, t * P:(t + 1) * P]).then_inc(misc_full, 1)

            def all_y_T(done):
                free(done)
                transposes(lambda t: y_tok[:, t, :]).then_inc(misc_full, 1)

            def project_out(b, done):
                free(done)
                pe.wait_ge(wp_ga_ready, b.n + 1)
                for t in range(TT):
                    last = pe.matmul(misc[:, t * P:(t + 1) * P], yT[:, t * P:(t + 1) * P], wp_ga[:], start=True, stop=True)
                last.then_inc(misc_full, 1)

            def h2_T(b, done):
                free(done)
                pe.wait_ge(h2_ready, K_TOP * b.n + 1)
                transposes(lambda t: rec[b.par][:, 0, t, 0:C]).then_inc(misc_full, 1)

            def router_logits(done):
                free(done)
                for t in range(TT):
                    last = pe.matmul(misc[:, t * E:(t + 1) * E], h2T_now[:, t * P:(t + 1) * P], router_T[:],
                                     start=True, stop=True)
                last.then_inc(misc_full, 1)

            def ranks(b, done):
                free(done)
                pe.wait_ge(marks_ready, b.n + 1)
                pe.matmul(misc[:, 0:(TT + 1) * E], before[:], marks[:].rearrange("p t e -> p (t e)"), start=True, stop=True)
                for t in range(TT):
                    last = pe.matmul(misc[:, (t + 1) * E:(TT + 1) * E], ones_bf[:],
                                     marks[:, t:t + 1, :].to_broadcast([P, TT - t, E]), start=False, stop=True,
                                     skip_group_check=True)
                last.then_inc(misc_full, 1)

            def max_scores(b, g, hh, half):
                h = HG * g + hh
                fill = 2 * HG * (G * b.n + g) + 2 * hh + half
                if b.const > 0 or g > 0 or hh > 0:
                    pe.wait_ge(mx_free, fill - 1)
                for t in range(2):
                    q0 = (2 * half + t) * P
                    last = pe.matmul(mx_bank[half][:, t, :], qs[b.par][0:MROW, h, q0:q0 + P], ks[b.par][0:MROW, h, :],
                                     start=True, stop=True)
                last.then_inc(mx_full, 1)

            def scores(b, n, hh):
                h, j = HG * (n // TT) + hh, n % TT
                fill = HG * (SLOTS * b.n + n) + hh
                if b.const > 0 or n > 0 or hh >= 2:
                    pe.wait_ge(exp_done, fill - 1)
                pe.matmul(st_bank[hh % 2][:], ks[b.par][:, h, j * P:(j + 1) * P], qs[b.par][:, h, :],
                          start=True, stop=True).then_inc(st_full, 1)

            def products(b, n):
                g, j = n // TT, n % TT
                quad = SLOTS * b.n + n
                pe.wait_ge(exp_done, HG * (quad + 1))
                if j == 0 and (b.const > 0 or g > 0):
                    pe.wait_ge(y_evacuated, G * b.n + g)
                for hh in range(HG):
                    last = pe.matmul(pv_bank[32 * hh:32 * (hh + 1), :], vs[b.par][:, j, HG * g + hh, :], pt[n % 2][:, hh, :],
                                     start=(j == 0), stop=(j == TT - 1))
                last.then_inc(pv_done, 1)

            ln1_T(B0, use(AHEAD, "ln1_0"))
            project(0, use(AHEAD, "q_0"))
            project(1, use(AHEAD, "k_0"))
            project_v(use(AHEAD, "v_0"))
            ln1_T(B1, use(AHEAD, "ln1_1"))
            project(0, use(AHEAD, "q_1"))
            project(1, use(AHEAD, "k_1"))
            pe.wait_ge(silu_spread, 1)
            for b in range(B):
                if b >= 4:
                    pe.wait_ge(bc_free, 4 * (b - 3))
                pe.matmul(mx_bank[(b // 2) % 2][:, b % 2, :], silu_bc[:, b, :], wmod_sb[:, 2 * C:6 * C],
                          start=True, stop=True).then_inc(bc_full, 1)
            pe.wait_ge(bc_free, 4 * B)
            pe.wait_ge(stack_loaded[0], STACK_DMAS)
            for g in range(2):
                for hh in range(HG):
                    for half in range(2):
                        max_scores(B0, g, hh, half)
            max_T(B0, 0, use(AHEAD, "m0"))
            free(use(AHEAD, "shared1"))
            pe.wait_ge(shared_loaded, 48)
            transposes(lambda i: nat[:, i, :]).then_inc(misc_full, 1)
            free(use(AHEAD, "shared2"))
            for j in range(IC):
                last = pe.transpose(misc[:, j * P:(j + 1) * P], nat[:, 4 + j, :], ident[:])
            last.then_inc(misc_full, 1)

            def body(b, first, last):
                for n in range(SLOTS):
                    g, j = n // TT, n % TT
                    ahead = n < 8 or not last
                    ahead_b, ahead_g = group_ahead(b, g)
                    if j == 0:
                        pe.wait_ge(m_row_loaded[g % 2], 16 * (2 * b.n + g // 2 + 1))
                    if n == 8 and not last:
                        nb = b.plus(1)
                        pe.wait_ge(stack_loaded[nb.par], STACK_DMAS * (nb.half + 1))
                    scores(b, n, 0)
                    scores(b, n, 1)
                    if ahead:
                        max_scores(ahead_b, ahead_g, j, 0)
                    scores(b, n, 2)
                    if ahead:
                        max_scores(ahead_b, ahead_g, j, 1)
                    scores(b, n, 3)
                    if n > 0:
                        products(b, n - 1)
                    elif not first:
                        products(b.plus(-1), SLOTS - 1)
                    if n == 0:
                        max_T(b, 1, use(b, "m1"))
                    if n == 0 and not last:
                        project_v(use(b, "v"))
                    if n == 1 and not first:
                        y_T(b.plus(-1), G - 1, use(b, "y3"))
                    if n in (5, 9, 13):
                        y_T(b, n // 4 - 1, use(b, f"y{n // 4 - 1}"))
                    if n in (4, 8):
                        max_T(b, n // 4 + 1, use(b, f"m{n // 4 + 1}"))
                    if n == 2 and not first:
                        all_y_T(use(b, "yT"))
                    if n == 3 and not first:
                        project_out(b.plus(-1), use(b, "out"))
                    if n == 6 and not last:
                        ln1_T(b.plus(2), use(b, "ln1"))
                    if n == 7 and not first:
                        h2_T(b.plus(-1), use(b, "h2T"))
                    if n == 10 and not first:
                        router_logits(use(b, "lg"))
                    if n == 11 and not last:
                        project(0, use(b, "q"))
                    if n == 12 and not last:
                        max_T(b.plus(1), 0, use(b, "m0"))
                    if n == 14 and not last:
                        project(1, use(b, "k"))
                    if n == 15 and not first:
                        ranks(b.plus(-1), use(b, "rank"))

            batches(pe, body)
            def shared_up(b):
                for j in range(IC):
                    if b >= 1:
                        pe.wait_ge(s_act, IC * (b - 1) + j + 1)
                    for which in range(2):
                        last = pe.matmul(mx_bank[j][:, which, :], shared_w[:, IC * which + j, :], h2T[:, T * b:T * (b + 1)],
                                         start=True, stop=True)
                    last.then_inc(s_full, 1)

            def shared_dn(b):
                pe.wait_ge(s_act, IC * (b + 1))
                if b >= 2:
                    pe.wait_ge(s_out, b - 1)
                for t in range(TT):
                    for j in range(IC):
                        last = pe.matmul(st_bank[b % 2][:, t * P:(t + 1) * P], act_s[:, b % 2, j, t * P:(t + 1) * P],
                                         shared_down[:, j, :], start=(j == 0), stop=(j == IC - 1))
                last.then_inc(s_down, 1)

            products(B_LAST, SLOTS - 1)
            pe.wait_ge(mx_free, 2 * HG * G * B)
            shared_up(0)
            y_T(B_LAST, G - 1, use(B_LAST, "y3_last"))
            shared_up(1)
            shared_dn(0)
            all_y_T(use(B_LAST, "yT_last"))
            shared_up(2)
            project_out(B_LAST, use(B_LAST, "out_last"))
            shared_dn(1)
            shared_up(3)
            shared_dn(2)
            shared_up(4)
            h2_T(B_LAST, use(B_LAST, "h2T_last"))
            shared_dn(3)
            router_logits(use(B_LAST, "lg_last"))
            shared_up(5)
            shared_dn(4)
            shared_up(6)
            ranks(B_LAST, use(B_LAST, "rank_last"))
            shared_dn(5)
            shared_up(7)
            shared_dn(6)
            shared_dn(7)

            def experts_of(turn):
                packed = pe.value_load(turn_experts[0:1, bass.ds(turn, 1)], min_val=0, max_val=E ** RING - 1)
                return [(packed >> (3 * k)) & (E - 1) for k in range(RING)]

            def unit_T(u, slot, turn):
                pe.wait_ge(xu_loaded[slot], 16 * (turn + 1))
                pe.transpose(mx_bank[0][:, slot % 2, 0:P], xu[slot][:, 0:C], ident[:]).then_inc(xuT_full, 1)

            def unit_up(u, slot, e, wait):
                pe.wait_ge(xuT_ready, u + 1)
                if wait:
                    pe.wait_ge(act_ready, u - 1)
                pe.matmul(st_bank[slot % 2][:], xuT[slot % 2], gate_up[:, bass.ds(e, 1), :].rearrange("p o i -> p (o i)"),
                          start=True, stop=True).then_inc(gu_full, 1)

            def unit_actT(u, slot, wait):
                pe.wait_ge(act_ready, u + 1)
                if wait:
                    pe.wait_ge(actT_ready, u - 1)
                for j in range(IC):
                    last = pe.transpose(mx_bank[1][:, slot % 2, j * P:(j + 1) * P], act_u[slot % 2][:, j * P:(j + 1) * P], ident[:])
                last.then_inc(actT_full, 1)

            def unit_dn(u, slot, e, wait):
                pe.wait_ge(actT_ready, u + 1)
                if wait:
                    pe.wait_ge(yu_ready, u - 1)
                for j in range(IC):
                    last = pe.matmul((pv_bank, misc)[slot % 2][:, 0:C], actT_u[slot % 2][:, j * P:(j + 1) * P],
                                     down[:, bass.ds(e, 1), j, :].rearrange("p o c -> p (o c)"), start=(j == 0), stop=(j == IC - 1))
                last.then_inc(yu_full, 1)

            def unit_step(i, k, turn, experts, earlier_turn=None, has_up=True, has_T=True, has_actT=True, has_dn=True, waits=3):
                if has_up:
                    unit_up(i, k % RING, experts[k], waits > 0)
                if has_actT:
                    unit_actT(i - 1, (k - 1) % RING, waits > 1)
                if has_T:
                    unit_T(i + 1, (k + 1) % RING, turn + (k + 1) // RING)
                if has_dn:
                    unit_dn(i - 2, (k - 2) % RING, (experts if k >= 2 else earlier_turn)[(k - 2) % RING], waits > 2)

            pe.wait_ge(routed_loaded, 64)
            pe.wait_ge(tables_ready, 3)
            unit_T(0, 0, 0)
            pe.wait_ge(s_out, B)
            experts = experts_of(0)
            for i in range(RING):
                unit_step(i, i, 0, experts, has_actT=i >= 1, has_dn=i >= 2, waits=max(i - 1, 0))
            with pe.Fori(1, UNITS // RING - 1) as it:
                earlier_turn, experts = experts_of(it - 1), experts_of(it)
                for k in range(RING):
                    unit_step(RING * it + k, k, it, experts, earlier_turn)
            earlier_turn, experts = experts_of(UNITS // RING - 2), experts_of(UNITS // RING - 1)
            for k in range(RING + 2):
                i = UNITS - RING + k
                unit_step(i, k, UNITS // RING - 1, experts, earlier_turn, has_up=i < UNITS, has_T=i + 1 < UNITS, has_actT=i - 1 < UNITS)


_INS = ["L0_attn_x", "L0_attn_Wq", "L0_attn_bq", "L0_attn_Wk", "L0_attn_bk", "L0_attn_Wv", "L0_attn_bv",
        "L0_attn_Wp", "L0_attn_bp", "L0_ffn_shared_gate", "L0_ffn_shared_up", "L0_ffn_shared_down",
        "L0_ffn_gate_w", "L0_ffn_up_w", "L0_ffn_down_w", "L0_ffn_router_w", "L0_ffn_routing_bias",
        "L0_c", "L0_wmod"]


def kernel(**inputs):
    import numpy as np
    import concourse.bacc as bacc
    from concourse.bass_utils import run_bass_kernel_spmd

    nc = bacc.Bacc("TRN2", target_bir_lowering=False, num_devices=1)
    arrays, args = {}, []
    for name in _INS:
        a = np.ascontiguousarray(inputs[name])
        arrays[name] = a
        args.append(nc.dram_tensor(name, a.shape, mybir.dt.from_np(a.dtype), kind="ExternalInput").ap())
    out = nc.dram_tensor("out", (B, T, C), F32, kind="ExternalOutput").ap()
    adaln_block(nc, *args, out)
    return run_bass_kernel_spmd(nc, [arrays], core_ids=[0]).results[0]["out"]
```

```python
from contextlib import ExitStack

import concourse.bass as bass
from concourse import mybir

ALU = mybir.AluOpType
ACT = mybir.ActivationFunctionType
AX_X = mybir.AxisListType.X
F32 = mybir.dt.float32
BF16 = mybir.dt.bfloat16

P = 128
B, T, C = 8, 512, 128
H = 16
DH = C // H
TT = T // P
HG = 4
G = H // HG
SLOTS = G * TT
E, I = 8, 256
IC = I // P
PARTS = 3
PROD = PARTS * PARTS * DH
MROW = 96
SCALE = float(DH) ** -0.5
EPS = 1e-5
U32 = mybir.dt.uint32
I32 = mybir.dt.int32
TOKENS = B * T
K_TOP = 2
REC = C + 2
REGION = TOKENS + P
UNITS = K_TOP * TOKENS // P + E
RING = 8
FAR = 1 << 20


def adaln_block(nc: bass.Bass, x, Wq, bq, Wk, bk, Wv, bv, Wp, bp, sh_gate, sh_up, sh_down,
                gate_w, up_w, down_w, router_w, routing_bias, c, wmod, out):
    ctx = ExitStack()
    with ctx:
        def sb(name, shape, dt=F32):
            return ctx.enter_context(nc.sbuf_tensor(name, shape, dt))

        def psum(name, shape):
            return ctx.enter_context(nc.psum_tensor(name, shape, F32))

        def sem(name):
            return ctx.enter_context(nc.semaphore(name))

        st_bank = [psum(f"st{i}", [P, T]) for i in range(2)]
        mx_bank = [psum(f"mx{i}", [P, 2, T]) for i in range(2)]
        pv_bank = psum("pv", [P, T])
        misc = psum("misc", [P, T])
        misc_bf = misc[:, :].bitcast(BF16)

        qs = [sb(f"qs{i}", [P, H, T], BF16) for i in range(2)]
        ks = [sb(f"ks{i}", [P, H, T], BF16) for i in range(2)]
        vs = [sb(f"vs{i}", [P, TT, H, 32]) for i in range(2)]
        pt = [sb(f"pt{i}", [P, HG, T]) for i in range(2)]
        gate_up = qs[0][:].rearrange("p h t -> p (h t)").bitcast(F32).rearrange("p (e i) -> p e i", e=E)
        down = ks[0][:].rearrange("p h t -> p (h t)").bitcast(F32)[:, 0:E * I].rearrange("p (e j c) -> p e j c", e=E, j=IC)
        scratch = [b[:].rearrange("p h t -> p (h t)") for b in pt]
        w_sgn = scratch[0][:, 0:4 * C].rearrange("p (i c) -> p i c", c=C)
        w_neg = scratch[0][:, 4 * C:8 * C].rearrange("p (i c) -> p i c", c=C)
        nat = scratch[0][:, 8 * C:14 * C].rearrange("p (j c) -> p j c", c=C)
        silu_bc = scratch[1][:, 0:B * P].rearrange("p (b q) -> p b q", q=P)
        gate_sign = scratch[1][:, B * P:2 * B * P].rearrange("p (b c) -> p b c", c=C)
        ident = sb("ident", [P, P])
        ident_bf = sb("ident_bf", [P, P], BF16)
        w_nat = sb("w_nat", [P, 4, C])
        alpha = sb("alpha", [P, 4])
        wT = sb("wT", [P, 4, C])
        bias_qkv = sb("bias_qkv", [P, 3])
        silu_T = sb("silu_T", [P, B])
        wmod_sb = sb("wmod_sb", [P, 6 * C])
        mod_T = sb("mod_T", [P, 2, B])
        bp_bc = sb("bp_bc", [P, C])
        ga_bc = sb("ga_bc", [P, B, C])
        gb_bc = sb("gb_bc", [P, B, C])
        sb_bc = sb("sb_bc", [P, B, C])
        cb_bc = sb("cb_bc", [P, B, C])
        x_in = sb("x_in", [P, TT, C])
        x_ep = sb("x_ep", [P, TT, C])
        ln1 = sb("ln1", [P, TT, C])
        hT = sb("hT", [P, T])
        qk_f = [sb(f"qk_f{i}", [P, T]) for i in range(2)]
        qk_r = sb("qk_r", [P, T])
        qk_parts = [sb(f"qk_parts{i}", [P, PARTS, T], BF16) for i in range(2)]
        neg_max = [sb(f"neg_max{i}", [P, HG, TT]) for i in range(2)]
        m_rest = sb("m_rest", [P, HG * TT])
        m_parts = sb("m_parts", [P, PARTS, HG * TT], BF16)
        m_rows = [sb(f"m_rows{i}", [PARTS * HG * TT, P], BF16) for i in range(2)]
        y_strips = sb("y_strips", [P, T])
        y_rden = sb("y_rden", [P, TT, HG])
        y_tok = sb("y_tok", [P, TT, C])
        yT = sb("yT", [P, T])
        wp_ga = sb("wp_ga", [P, C])
        bp_ga = sb("bp_ga", [P, C])
        c_nat = sb("c_nat", [B, C])
        h2T = sb("h2T", [P, B * T])
        h2T_now = sb("h2T_now", [P, T])
        router_nat = sb("router_nat", [E, C])
        router_T = sb("router_T", [P, E])
        router_bias = sb("router_bias", [P, E])
        shared_w = sb("shared_w", [P, 4, P])
        shared_down = sb("shared_down", [P, IC, C])
        expert_no = sb("expert_no", [P, E])
        earlier_token = sb("earlier_token", [P, P], BF16)
        ones_bf = sb("ones_bf", [P, P], BF16)
        logits = sb("logits", [P, TT, E])
        probs = sb("probs", [P, TT, E])
        top_p = sb("top_p", [P, TT, 8])
        top_e = sb("top_e", [P, TT, 8], U32)
        top_ef = sb("top_ef", [P, TT, K_TOP])
        p_sum = sb("p_sum", [P, TT])
        p_rsum = sb("p_rsum", [P, TT])
        chosen = sb("chosen", [P, K_TOP, TT, E])
        marks = sb("marks", [P, TT + 1, E], BF16)
        place = sb("place", [P, TT, E])
        next_row = [sb(f"next_row{i}", [P, E]) for i in range(2)]
        picked = sb("picked", [P, K_TOP, TT, E])
        row_f = sb("row_f", [P, K_TOP, TT])
        row_u = sb("row_u", [P, K_TOP, TT], U32)
        home = sb("home", [P, K_TOP, TT])
        stats1_sb = sb("stats1_sb", [P, TT, 6])
        mv1 = sb("mv1", [P, TT, 2])
        rstd1 = sb("rstd1", [P, TT])
        stats2_sb = sb("stats2_sb", [P, TT, 6])
        mv2 = sb("mv2", [P, TT, 2])
        rstd2 = sb("rstd2", [P, TT])
        ve1 = sb("ve1", [P, TT])
        ve2 = sb("ve2", [P, TT])
        minus_half = sb("minus_half", [P, TT])
        ln2 = sb("ln2", [P, TT, C])
        rec = [sb(f"rec{i}", [P, K_TOP, TT, REC]) for i in range(2)]
        x1 = sb("x1", [P, B * TT, C])

        pad_row = sb("pad_row", [P, REC])
        first_row = sb("first_row", [P, E])
        unit_start = sb("unit_start", [P, UNITS])
        earlier = sb("earlier", [P, E, E])
        padded = sb("padded", [P, E])
        padded_i = sb("padded_i", [P, E], I32)
        region_end = sb("region_end", [P, E])
        skip = sb("skip", [P, E])
        entered = sb("entered", [P, UNITS, E])
        skipped = sb("skipped", [P, UNITS, E])
        unit_f = sb("unit_f", [P, 2, UNITS])
        unit_row = sb("unit_row", [P, UNITS], I32)
        digit = sb("digit", [P, RING])
        digits = sb("digits", [P, UNITS // RING, RING])
        packed_f = sb("packed_f", [P, UNITS // RING])
        turn_experts = sb("turn_experts", [P, UNITS // RING], I32)
        end_row = sb("end_row", [P, E], I32)
        silu_s = pt[0][:, 0:IC, :]
        act_s = pt[1][:].rearrange("p (b j) t -> p b j t", b=2)
        gated = pt[0][:, 2, :].rearrange("p (t c) -> p t c", t=TT)
        odd_q, odd_k = (b[1][:].rearrange("p h t -> p (h t)").bitcast(F32) for b in (qs, ks))
        xu = [odd_k[:, i * REC:(i + 1) * REC] for i in range(RING)]
        y_u = [odd_q[:, i * C:(i + 1) * C] for i in range(RING)]
        w_u = [odd_q[:, RING * C + i:RING * C + i + 1] for i in range(RING)]
        home_u = sb("home_u", [P, RING], U32)
        unit_a = vs[0][:].rearrange("p t h d -> p (t h d)")
        unit_b = vs[1][:].rearrange("p t h d -> p (t h d)")
        xuT = [unit_a[:, i * P:(i + 1) * P] for i in range(2)]
        silu_u = [unit_a[:, 2 * P + i * I:2 * P + (i + 1) * I] for i in range(2)]
        act_u = [unit_b[:, i * I:(i + 1) * I] for i in range(2)]
        actT_u = [unit_b[:, (2 + i) * I:(3 + i) * I] for i in range(2)]
        results = [[(odd_q, odd_k)[b // (B // 2)][:, (2 * (b % (B // 2)) + k) * T:(2 * (b % (B // 2)) + k + 1) * T]
                    .rearrange("p (t c) -> p t c", t=TT) for k in range(K_TOP)] for b in range(B)]

        q_dram = nc.dram_tensor("q_parts", (PARTS, DH, H, T), BF16).ap()
        routed_dram = nc.dram_tensor("routed", (E * REGION + P, REC), F32).ap()
        result_dram = nc.dram_tensor("results", (K_TOP * TOKENS, C), F32).ap()
        k_dram = nc.dram_tensor("k_parts", (PARTS, DH, H, T), BF16).ap()

        w_loaded = sem("w_loaded")
        small_loaded = sem("small_loaded")
        c_loaded = sem("c_loaded")
        consts_ready = sem("consts_ready")
        setup_dve = sem("setup_dve")
        setup_pool = sem("setup_pool")
        x_in_loaded = sem("x_in_loaded")
        x_ep_loaded = sem("x_ep_loaded")
        stats1_ready = sem("stats1_ready")
        rstd1_ready = sem("rstd1_ready")
        ln1_ready = sem("ln1_ready")
        first_ready = sem("first_ready")
        rest_ready = sem("rest_ready")
        parts_ready = sem("parts_ready")
        q_stored = sem("q_stored")
        k_stored = sem("k_stored")
        stacks_cleared = [sem(f"stacks_cleared{i}") for i in range(2)]
        var1_ready = sem("var1_ready")
        var2_ready = sem("var2_ready")
        m_chain = sem("m_chain")
        h2_chain = sem("h2_chain")
        home_ready = sem("home_ready")
        sig_exp = sem("sig_exp")
        route_chain = sem("route_chain")
        marks_ready = sem("marks_ready")
        rank_chain = sem("rank_chain")
        rows_ready = sem("rows_ready")
        weights_ready = sem("weights_ready")
        scattered = sem("scattered")
        rows_free = sem("rows_free")
        shared_loaded = sem("shared_loaded")
        routed_loaded = sem("routed_loaded")
        bp_ga_ready = sem("bp_ga_ready")
        stack_loaded = [sem(f"stack_loaded{i}") for i in range(2)]
        misc_full = sem("misc_full")
        misc_free = sem("misc_free")
        mx_full = sem("mx_full")
        mx_free = sem("mx_free")
        m_split = sem("m_split")
        m_row_loaded = [sem(f"m_row_loaded{i}") for i in range(2)]
        st_full = sem("st_full")
        exp_done = sem("exp_done")
        pv_done = sem("pv_done")
        y_evacuated = sem("y_evacuated")
        rden_ready = sem("rden_ready")
        xres_ready = sem("xres_ready")
        wp_ga_ready = sem("wp_ga_ready")
        stats2_ready = sem("stats2_ready")
        rstd2_ready = sem("rstd2_ready")
        ln2_ready = sem("ln2_ready")
        h2_ready = sem("h2_ready")
        out_stored = sem("out_stored")
        s_full = sem("s_full")
        s_silu = sem("s_silu")
        s_act = sem("s_act")
        s_down = sem("s_down")
        s_gated = sem("s_gated")
        s_out = sem("s_out")
        table_chain = sem("table_chain")
        tables_ready = sem("tables_ready")
        padding_written = sem("padding_written")
        xu_loaded = [sem(f"xu_loaded{i}") for i in range(RING)]
        xu_read = sem("xu_read")
        xuT_full = sem("xuT_full")
        xuT_ready = sem("xuT_ready")
        gu_full = sem("gu_full")
        silu_ready = sem("silu_ready")
        act_ready = sem("act_ready")
        actT_full = sem("actT_full")
        actT_ready = sem("actT_ready")
        yu_full = sem("yu_full")
        yu_ready = sem("yu_ready")
        yu_sent = [sem(f"yu_sent{i}") for i in range(RING)]
        results_loaded = [sem(f"results_loaded{i}") for i in range(B)]
        results_added = sem("results_added")
        out_ready = sem("out_ready")
        out_chain = sem("out_chain")
        pad_ready = sem("pad_ready")
        stats1_chain = sem("stats1_chain")
        stats2_chain = sem("stats2_chain")
        v_cleared = sem("v_cleared")
        bc_full = sem("bc_full")
        bc_free_dve = sem("bc_free_dve")
        bc_free_act = sem("bc_free_act")
        keys_cleared = sem("keys_cleared")
        gate_chain = sem("gate_chain")
        gates_ready = sem("gates_ready")
        gb_ready = sem("gb_ready")
        silu_spread = sem("silu_spread")
        held = {e: sem(f"held_{n}") for n, e in (("sp", nc.sync.engine), ("pool", nc.gpsimd.engine), ("dve", nc.vector.engine),
                                                 ("pe", nc.tensor.engine))}

        BEFORE = ["wT", "c", "mod", "ln1_0", "q_0", "k_0", "v_0", "ln1_1", "q_1", "k_1", "shared1", "shared2", "m0"]
        AT_SLOT = [["v"], ["m1"], ["y3"], ["yT"], ["out"], ["m2"], ["y0"], ["ln1"], ["q"], ["m3"], ["h2T"], ["y1"],
                   ["lg", "m0"], ["y2"], ["k"], ["rank"]]
        STEADY = [u for slot in AT_SLOT for u in slot]
        OF_BEFORE = ("y3", "yT", "out", "h2T", "lg", "rank")
        OF_AFTER = ("v", "ln1", "q", "k", "m0")
        FIRST = [u for u in STEADY if u not in OF_BEFORE]
        LAST = [u for u in STEADY if u not in OF_AFTER]
        LAST += [u + "_last" for u in OF_BEFORE]

        class Batch:

            def __init__(self, const, it=0):
                self.const, self.it = const, it
                self.n = 2 * it + const
                self.par = const % 2
                self.half = it + const // 2

            def plus(self, k):
                return Batch(self.const + k, self.it)

        def use(b, what):
            if b.const == -1:
                return BEFORE.index(what)
            if b.const == 0:
                return len(BEFORE) + FIRST.index(what)
            steady = len(BEFORE) + len(FIRST) + (b.n - 1) * len(STEADY)
            return steady + (LAST if b.const == B - 1 else STEADY).index(what)

        STACK_DMAS = 16 * (1 + PARTS)
        BATCH_ROWS = 16 * K_TOP * TT
        CHOOSE_STEPS = 2 + 2 * TT + 3 + 1
        AHEAD, B0, B1, B_LAST = Batch(-1), Batch(0), Batch(1), Batch(B - 1)

        def batches(eng, body):
            body(B0, True, False)
            with eng.Fori(0, (B - 2) // 2) as it:
                for k in (1, 2):
                    body(Batch(k, it), False, False)
            body(B_LAST, False, True)

        def wide(b, n):
            return b.const == B - 1 and n >= SLOTS // 2

        def score_bank(b, n, hh):
            if wide(b, n) and hh >= 2:
                return mx_bank[1][:, hh % 2, :]
            return st_bank[hh % 2][:]

        def group_ahead(b, g):
            return (b, g + 2) if g + 2 < G else (b.plus(1), g + 2 - G)

        def first_part(dve, b, i, done):
            if b.const > 0:
                dve.wait_ge((q_stored, k_stored)[i], 48 * b.n)
            dve.wait_ge(misc_free, done + 1)
            dve.tensor_copy(qk_parts[i][:, 0, :], qk_f[i][:]).then_inc(first_ready, 1)

        def split_qk(eng, b, i):
            parts, f = qk_parts[i], qk_f[i]
            eng.wait_ge(first_ready, 2 * b.n + i + 1)
            if b.const > 0 or i > 0:
                eng.wait_ge(parts_ready, 2 * b.n + i)
            eng.tensor_tensor(qk_r[:], f[:], parts[:, 0, :], ALU.subtract).then_inc(rest_ready, 1)
            hold(eng, rest_ready, 4 * b.n + 2 * i + 1)
            eng.tensor_copy(parts[:, 1, :], qk_r[:]).then_inc(rest_ready, 1)
            eng.wait_ge(rest_ready, 4 * b.n + 2 * i + 2)
            eng.tensor_tensor(parts[:, 2, :], qk_r[:], parts[:, 1, :], ALU.subtract).then_inc(parts_ready, 1)

        two_ones = 1.0 + 0x3F80 * 2.0 ** -23

        def fill_fixed(eng, i):
            eng.memset(vs[i][:], 0.0).then_inc(v_cleared, 1)
            eng.wait_ge(v_cleared, i + 1)
            eng.memset(vs[i][:, :, :, DH], 1.0).then_inc(stacks_cleared[i], 1)
            eng.wait_ge(stacks_cleared[i], 2)
            eng.wait_ge(keys_cleared, i + 1)
            eng.memset(ks[i][MROW:MROW + PARTS].rearrange("p h t -> p (h t)").bitcast(F32), two_ones).then_inc(stacks_cleared[i], 1)

        def hold(eng, sem_, value):
            eng.wait_ge(sem_, value)
            eng.sem_inc(held[eng.engine], 1)

        block = ctx.enter_context(nc.Block())

        @block.sync
        def _(sp):
            for i, w in enumerate((Wq, Wk, Wv, Wp)):
                sp.dma_start(w_nat[:, i, :], w).then_inc(w_loaded, 16)
            sp.dma_start(x_in[:], x[0].rearrange("(t p) c -> p t c", p=P)).then_inc(x_in_loaded, 16)
            sp.dma_start(c_nat[:], c).then_inc(c_loaded, 16)
            for i, v in enumerate((bq, bk, bv)):
                sp.dma_start(bias_qkv[:, i:i + 1], v.rearrange("(p o) -> p o", o=1)).then_inc(small_loaded, 16)
            sp.dma_start(bp_bc[:], bp.partition_broadcast(P)).then_inc(small_loaded, 16)
            sp.dma_start(router_nat[:], router_w).then_inc(c_loaded, 16)
            sp.dma_start(router_bias[:], routing_bias.partition_broadcast(P)).then_inc(small_loaded, 16)
            sp.dma_start(nat[:, 0:2, :], sh_gate.rearrange("(j p) c -> p j c", p=P)).then_inc(shared_loaded, 16)
            sp.dma_start(nat[:, 2:4, :], sh_up.rearrange("(j p) c -> p j c", p=P)).then_inc(shared_loaded, 16)
            sp.dma_start(nat[:, 4:6, :], sh_down.rearrange("c (j i) -> c j i", j=IC)).then_inc(shared_loaded, 16)

            def load_x(b):
                sp.wait_ge(ln1_ready, TT * b.n)
                sp.dma_start(x_in[:], x[bass.ds(b.n % B, 1)].rearrange("o (t p) c -> p (o t) c", p=P)).then_inc(x_in_loaded, 16)

            def store_parts(b):
                for i, (parts, dram, stored) in enumerate(((qk_parts[0], q_dram, q_stored), (qk_parts[1], k_dram, k_stored))):
                    if b.const > 0:
                        before = b.plus(-1)
                        hold(sp, stack_loaded[before.par], STACK_DMAS * (before.half + 1))
                    sp.wait_ge(parts_ready, 2 * b.n + i + 1)
                    for j in range(PARTS):
                        sp.dma_start(dram[j].rearrange("d h t -> h d t"), parts[:, j, :]).then_inc(stored, 16)

            def load_stacks(b):
                if b.const >= 2:
                    hold(sp, pv_done, SLOTS * (b.n - 1))
                else:
                    sp.wait_ge(stacks_cleared[b.par], 3)
                sp.wait_ge(q_stored, 48 * (b.n + 1))
                sp.wait_ge(k_stored, 48 * (b.n + 1))
                sp.dma_start(qs[b.par][0:PROD],
                             q_dram.rearrange("i d h t -> (i d) (h t)").unsqueeze(0).to_broadcast([PARTS, PARTS * DH, H * T])
                             ).then_inc(stack_loaded[b.par], 16)
                for j in range(PARTS):
                    r = j * PARTS * DH
                    sp.dma_start(ks[b.par][r:r + PARTS * DH],
                                 k_dram[j].rearrange("d h t -> d (h t)").unsqueeze(0).to_broadcast([PARTS, DH, H * T])
                                 ).then_inc(stack_loaded[b.par], 16)

            def load_x_again(b):
                if b.const > 0:
                    sp.wait_ge(stats2_ready, TT * b.n)
                sp.dma_start(x_ep[:], x[bass.ds(b.n, 1)].rearrange("o (t p) c -> p (o t) c", p=P)).then_inc(x_ep_loaded, 16)

            load_x(B1)
            store_parts(B0)
            load_stacks(B0)
            load_x(B1.plus(1))
            store_parts(B1)
            def body(b, first, last):
                if not last:
                    load_stacks(b.plus(1))
                load_x_again(b)
                if not last:
                    load_x(b.plus(3))
                    store_parts(b.plus(2))

            batches(sp, body)
            sp.wait_ge(pv_done, SLOTS * (B - 1))
            sp.dma_start(gate_up[:, :, 0:I], gate_w.rearrange("e c i -> c e i")).then_inc(routed_loaded, 16)
            sp.dma_start(gate_up[:, :, I:2 * I], up_w.rearrange("e c i -> c e i")).then_inc(routed_loaded, 16)
            for j in range(IC):
                sp.dma_start(down[:, :, j, :], down_w[:, j * P:(j + 1) * P, :].rearrange("e i c -> i e c")).then_inc(routed_loaded, 16)
            sp.wait_ge(pad_ready, 2)
            sp.dma_start(routed_dram[E * REGION:E * REGION + P, :], pad_row[:]).then_inc(padding_written, 16)
            sp.wait_ge(tables_ready, 1)
            for e in range(E):
                row = sp.value_load(end_row[0:1, e:e + 1], min_val=e * REGION, max_val=e * REGION + TOKENS)
                sp.dma_start(routed_dram[bass.ds(row, P), :], pad_row[:]).then_inc(padding_written, 16)
            sp.wait_ge(padding_written, 16 * (E + 1))
            sp.wait_ge(scattered, BATCH_ROWS * B)
            sp.wait_ge(tables_ready, 3)

            def load_unit(u, slot, wait):
                row = sp.value_load(unit_row[0:1, bass.ds(u, 1)], min_val=0, max_val=E * REGION)
                if wait:
                    sp.wait_ge(xu_read, u - RING + 1)
                    sp.wait_ge(xuT_full, u - RING + 1)
                sp.dma_start(xu[slot], routed_dram[bass.ds(row, P), :]).then_inc(xu_loaded[slot], 16)

            for u in range(RING):
                load_unit(u, u, False)
            with sp.Fori(1, UNITS // RING) as it:
                for slot in range(RING):
                    load_unit(RING * it + slot, slot, True)

            for slot in range(RING):
                sp.wait_ge(yu_sent[slot], 16 * UNITS // RING)
            result_v = result_dram.rearrange("(k b t p) c -> p k b t c", k=K_TOP, b=B, p=P)
            out_v = out.rearrange("b (t p) c -> p b t c", p=P)
            for b in range(B):
                for k in range(K_TOP):
                    sp.dma_start(results[b][k], result_v[:, k, b]).then_inc(results_loaded[b], 16)
            for b in range(B):
                sp.wait_ge(out_ready, b + 1)
                sp.dma_start(out_v[:, b], x1[:, TT * b:TT * (b + 1), :]).then_inc(out_stored, 16)
            sp.wait_ge(out_stored, 16 * B)
            sp.wait_ge(q_stored, 48 * (B + 1))
            sp.wait_ge(k_stored, 48 * (B + 1))

        @block.gpsimd
        def _(pool):
            pool.memset(ident[:], 0.0).then_inc(setup_pool, 1)
            pool.wait_ge(setup_pool, 1)
            pool.affine_select(out=ident[:], in_=ident[:], compare_op=ALU.not_equal, fill=1.0, base=0,
                               pattern=[[-1, P]], channel_multiplier=1).then_inc(consts_ready, 1)
            pool.wait_ge(consts_ready, 1)
            pool.tensor_copy(ident_bf[:], ident[:]).then_inc(consts_ready, 1)
            pool.memset(minus_half[:], -0.5).then_inc(setup_pool, 1)
            pool.memset(ones_bf[:], 1.0).then_inc(setup_pool, 1)
            pool.wait_ge(setup_pool, 3)
            pool.affine_select(out=earlier_token[:], in_=ones_bf[:], compare_op=ALU.is_gt, fill=0.0, base=0,
                               pattern=[[1, P]], channel_multiplier=-1).then_inc(consts_ready, 1)
            pool.memset(marks[:], 0.0).then_inc(consts_ready, 1)
            pool.sem_inc(rows_free, 2)
            pool.iota(expert_no[:], pattern=[[1, E]], base=0, channel_multiplier=0,
                      allow_small_or_imprecise_dtypes=True).then_inc(consts_ready, 1)
            pool.iota(next_row[0][:], pattern=[[REGION, E]], base=0, channel_multiplier=0,
                      allow_small_or_imprecise_dtypes=True).then_inc(consts_ready, 1)
            for k in range(RING):
                pool.memset(digit[:, k:k + 1], float(E ** k)).then_inc(consts_ready, 1)
            pool.memset(pad_row[:], 0.0).then_inc(pad_ready, 1)
            pool.wait_ge(pad_ready, 1)
            pool.memset(pad_row[:, C + 1:C + 2], float(FAR)).then_inc(pad_ready, 1)
            pool.iota(first_row[:], pattern=[[REGION, E]], base=0, channel_multiplier=0,
                      allow_small_or_imprecise_dtypes=True).then_inc(consts_ready, 1)
            pool.iota(unit_start[:], pattern=[[P, UNITS]], base=0, channel_multiplier=0,
                      allow_small_or_imprecise_dtypes=True).then_inc(consts_ready, 1)
            pool.affine_select(out=earlier[:], in_=ones_bf[:, 0:E * E].rearrange("p (e f) -> p e f", e=E), compare_op=ALU.is_gt,
                               fill=0.0, base=0, pattern=[[1, E], [-1, E]], channel_multiplier=0).then_inc(consts_ready, 1)
            pool.iota(home[:], pattern=[[TOKENS, K_TOP], [P, TT]], base=0, channel_multiplier=1,
                      allow_small_or_imprecise_dtypes=True).then_inc(setup_pool, 1)
            pool.memset(qs[0][:].rearrange("p h t -> p (h t)").bitcast(F32), 0.0).then_inc(stacks_cleared[0], 1)

            def rstd(mv, ve, ve_ready, out_, ready, stats_ready, b):
                hold(pool, stats_ready, TT * (b.n + 1))
                pool.tensor_scalar(ve[:], mv[:, :, 1], EPS, None, ALU.add).then_inc(ve_ready, 1)
                pool.wait_ge(ve_ready, b.n + 1)
                pool.tensor_tensor(out_[:], ve[:], minus_half[:], ALU.pow).then_inc(ready, 1)

            def residual(b):
                ga = ga_bc[:, bass.ds(b.n, 1), :].rearrange("p o c -> p (o c)")
                pool.tensor_tensor(bp_ga[:], bp_bc[:], ga, ALU.mult).then_inc(bp_ga_ready, 1)
                pool.tensor_tensor(wp_ga[:], wT[:, 3, :], ga, ALU.mult).then_inc(wp_ga_ready, 1)
                pool.wait_ge(bp_ga_ready, b.n + 1)
                pool.wait_ge(x_ep_loaded, 16 * (b.n + 1))
                pool.tensor_tensor(x_ep[:], x_ep[:], bp_ga[:].unsqueeze(1).to_broadcast([P, TT, C]),
                                   ALU.add).then_inc(xres_ready, 1)

            def modulate2(b):
                pool.wait_ge(ln2_ready, TT * (b.n + 1))
                pool.tensor_tensor(ln2[:], ln2[:], cb_bc[:, bass.ds(b.n, 1), :].to_broadcast([P, TT, C]),
                                   ALU.mult).then_inc(h2_chain, 1)
                pool.wait_ge(h2_chain, b.n + 1)
                pool.wait_ge(rows_free, b.n + 1)
                for k in range(K_TOP):
                    pool.tensor_tensor(rec[b.par][:, k, :, 0:C], ln2[:],
                                       sb_bc[:, bass.ds(b.n, 1), :].to_broadcast([P, TT, C]), ALU.add).then_inc(h2_ready, 1)
                pool.tensor_copy(rec[b.par][:, :, :, C + 1], home[:]).then_inc(home_ready, 1)
                hold(pool, home_ready, 2 * b.n + 1)
                pool.tensor_scalar(home[:], home[:], float(T), None, ALU.add).then_inc(home_ready, 1)

            def scatter(b):
                hold(pool, rows_ready, b.n + 1)
                for k in range(K_TOP):
                    for t in range(TT):
                        pool.indirect_dma_start(out=routed_dram, out_offset=bass.IndirectOffsetOnAxis(ap=row_u[:, k, t:t + 1], axis=0),
                                                in_=rec[b.par][:, k, t, :], in_offset=None).then_inc(scattered, 16)
                pool.wait_ge(scattered, BATCH_ROWS * (b.n + 1))
                pool.sem_inc(rows_free, 1)

            pool.wait_ge(setup_pool, 4)
            rstd(mv1, ve1, var1_ready, rstd1, rstd1_ready, stats1_ready, B0)
            pool.wait_ge(misc_free, use(AHEAD, "c") + 1)
            pool.tensor_copy(silu_bc, silu_T[:].unsqueeze(2).to_broadcast([P, B, P])).then_inc(silu_spread, 1)
            rstd(mv1, ve1, var1_ready, rstd1, rstd1_ready, stats1_ready, B1)
            pool.memset(qs[1][:].rearrange("p h t -> p (h t)").bitcast(F32), 0.0).then_inc(stacks_cleared[1], 1)
            fill_fixed(pool, 1)

            def body(b, first, last):
                if not last:
                    rstd(mv1, ve1, var1_ready, rstd1, rstd1_ready, stats1_ready, b.plus(2))
                if not first:
                    rstd(mv2, ve2, var2_ready, rstd2, rstd2_ready, stats2_ready, b.plus(-1))
                if not first:
                    modulate2(b.plus(-1))
                residual(b)
                if not last:
                    split_qk(pool, b.plus(2), 0)
                    split_qk(pool, b.plus(2), 1)
                if not first:
                    scatter(b.plus(-1))

            pool.wait_ge(gates_ready, 1)
            batches(pool, body)
            rstd(mv2, ve2, var2_ready, rstd2, rstd2_ready, stats2_ready, B_LAST)
            modulate2(B_LAST)
            scatter(B_LAST)

            def send_unit(u, slot):
                hold(pool, yu_ready, u + 1)
                pool.indirect_dma_start(out=result_dram, out_offset=bass.IndirectOffsetOnAxis(ap=home_u[:, slot:slot + 1], axis=0),
                                        in_=y_u[slot], in_offset=None, bounds_check=K_TOP * TOKENS - 1,
                                        oob_is_err=False).then_inc(yu_sent[slot], 16)

            with pool.Fori(0, UNITS // RING) as it:
                for slot in range(RING):
                    send_unit(RING * it + slot, slot)
            for b in range(B):
                r = results[b]
                pool.wait_ge(results_loaded[b], 16 * K_TOP)
                pool.tensor_tensor(r[0], r[0], r[1], ALU.add).then_inc(results_added, 1)

        @block.scalar
        def _(act):
            act.dma_start(wmod_sb[:], wmod).then_inc(c_loaded, 16)

            def clear_keys(i):
                act.activation(ks[i][:].rearrange("p h t -> p (h t)").bitcast(F32), ident[:, 0:1].to_broadcast([P, H * T // 2]),
                               ACT.Copy, scale=0.0).then_inc(keys_cleared, 1)

            act.wait_ge(consts_ready, 1)
            clear_keys(0)
            act.wait_ge(misc_full, use(AHEAD, "wT") + 1)
            act.activation(wT[:].rearrange("p i c -> p (i c)"), misc[:], ACT.Copy).then_inc(misc_free, 1)
            act.wait_ge(misc_full, use(AHEAD, "c") + 1)
            act.activation(router_T[:], misc[:, B:B + E], ACT.Copy)
            act.activation(silu_T[:], misc[:, 0:B], ACT.Silu).then_inc(misc_free, 1)
            act.wait_ge(misc_full, use(AHEAD, "mod") + 1)
            act.activation(mod_T[:, 0, :], misc[:, 0:B], ACT.Identity)
            act.activation(mod_T[:, 1, :], misc[:, B:2 * B], ACT.Identity, bias=1.0).then_inc(misc_free, 1)
            act.wait_ge(misc_free, use(AHEAD, "mod") + 1)
            act.wait_ge(small_loaded, 80)

            def project_in(b, done):
                act.wait_ge(misc_full, done + 1)
                nb = b.n % B
                act.activation(hT[:], misc[:], ACT.Identity, bias=mod_T[:, 0, bass.ds(nb, 1)],
                               scale=mod_T[:, 1, bass.ds(nb, 1)]).then_inc(misc_free, 1)

            def evacuate_qk(b, i, done):
                act.wait_ge(misc_full, done + 1)
                if b.const > 0:
                    act.wait_ge(parts_ready, 2 * (b.n - 1) + i + 1)
                act.activation(qk_f[i][:], misc[:], ACT.Identity, bias=bias_qkv[:, i:i + 1]).then_inc(misc_free, 1)

            def evacuate_v(b, done):
                act.wait_ge(misc_full, done + 1)
                act.activation(vs[b.par][:, :, :, 0:DH], misc[:].rearrange("p (t h d) -> p t h d", t=TT, d=DH),
                               ACT.Copy).then_inc(misc_free, 1)

            def max_rows(b, g, done):
                act.wait_ge(misc_full, done + 1)
                if b.const > 0 or g >= 2:
                    act.wait_ge(m_row_loaded[g % 2], 16 * (2 * b.n + g // 2))
                act.activation(m_rows[g % 2][:], misc_bf[0:PARTS * HG * TT, 0:P], ACT.Copy).then_inc(misc_free, 1)
                act.wait_ge(misc_free, done + 1)
                act.dma_start(qs[b.par][MROW:MROW + PARTS, HG * g:HG * (g + 1), :].rearrange("p h (t q) -> p (h t) q", t=TT),
                              m_rows[g % 2][:]).then_inc(m_row_loaded[g % 2], 16)

            def exponentials(b, n):
                quad = SLOTS * b.n + n
                if b.const > 0 or n >= 2:
                    act.wait_ge(pv_done, quad - 1)
                for hh in range(HG):
                    act.wait_ge(st_full, HG * quad + hh + 1)
                    act.activation(pt[n % 2][:, hh, :], score_bank(b, n, hh), ACT.Exp, scale=SCALE).then_inc(exp_done, 1)

            def evacuate_y(b, g):
                act.wait_ge(pv_done, SLOTS * b.n + TT * (g + 1))
                act.activation(y_strips[:], pv_bank[:], ACT.Copy).then_inc(y_evacuated, 1)

            def evacuate_yT(done):
                act.wait_ge(misc_full, done + 1)
                act.activation(yT[:], misc[:], ACT.Identity, bias=bias_qkv[:, 2:3]).then_inc(misc_free, 1)

            def evacuate_h2T(b, done):
                act.wait_ge(misc_full, done + 1)
                act.activation(h2T_now[:], misc[:], ACT.Copy)
                act.activation(h2T[:, bass.ds(T * b.n, T)], misc[:], ACT.Copy).then_inc(misc_free, 1)

            def exp_minus_logits(b, done):
                act.wait_ge(misc_free, done + 1)
                act.activation(probs[:], logits[:], ACT.Exp, scale=-1.0).then_inc(sig_exp, 1)

            project_in(B0, use(AHEAD, "ln1_0"))
            for i, w in enumerate("qk"):
                evacuate_qk(B0, i, use(AHEAD, w + "_0"))
            act.wait_ge(stacks_cleared[0], 3)
            evacuate_v(B0, use(AHEAD, "v_0"))
            clear_keys(1)
            for b in range(1, B, 2):
                act.wait_ge(bc_full, b + 1)
                for k, dst in enumerate((ga_bc, sb_bc, cb_bc, gb_bc)):
                    act.activation(dst[:, b, :], mx_bank[(b // 2) % 2][:, b % 2, k * C:(k + 1) * C], ACT.Copy,
                                   bias=1.0 if dst is cb_bc else 0.0).then_inc(bc_free_act, 1)
            project_in(B1, use(AHEAD, "ln1_1"))
            for i, w in enumerate("qk"):
                evacuate_qk(B1, i, use(AHEAD, w + "_1"))
            act.wait_ge(misc_full, use(AHEAD, "shared1") + 1)
            act.activation(shared_w[:].rearrange("p j i -> p (j i)"), misc[:], ACT.Copy).then_inc(misc_free, 1)
            act.wait_ge(misc_full, use(AHEAD, "shared2") + 1)
            act.activation(shared_down[:].rearrange("p j c -> p (j c)"), misc[:, 0:IC * C], ACT.Copy).then_inc(misc_free, 1)
            act.wait_ge(stacks_cleared[1], 3)
            max_rows(B0, 0, use(AHEAD, "m0"))

            def body(b, first, last):
                for n in range(SLOTS):
                    exponentials(b, n)
                    if n == 0 and not first:
                        evacuate_y(b.plus(-1), G - 1)
                    if n == 0 and not last:
                        evacuate_v(b.plus(1), use(b, "v"))
                    if n in (1, 5, 9):
                        max_rows(b, n // 4 + 1, use(b, f"m{n // 4 + 1}"))
                    if n == 8 and not last:
                        evacuate_qk(b.plus(2), 0, use(b, "q"))
                    if n == 3 and not first:
                        evacuate_yT(use(b, "yT"))
                    if n == 7 and not last:
                        project_in(b.plus(2), use(b, "ln1"))
                    if n == 10 and not first:
                        evacuate_h2T(b.plus(-1), use(b, "h2T"))
                    if n == 12 and not first:
                        exp_minus_logits(b.plus(-1), use(b, "lg"))
                    if n in (4, 8, 12):
                        if n > 4 or not first:
                            act.wait_ge(misc_full, use(b, ("y3", "y0", "y1")[n // 4 - 1]) + 1)
                        evacuate_y(b, n // 4 - 1)
                    if n == 12 and not last:
                        max_rows(b.plus(1), 0, use(b, "m0"))
                    if n == 14 and not last:
                        evacuate_qk(b.plus(2), 1, use(b, "k"))

            batches(act, body)
            def shared_silu(b, j):
                act.wait_ge(s_full, IC * b + j + 1)
                if b >= 1:
                    act.wait_ge(s_act, IC * (b - 1) + j + 1)
                act.activation(silu_s[:, j, :], mx_bank[j][:, 0, :], ACT.Silu).then_inc(s_silu, 1)

            act.wait_ge(misc_full, use(B_LAST, "y2") + 1)
            evacuate_y(B_LAST, G - 1)
            shared_silu(0, 0)
            shared_silu(0, 1)
            evacuate_yT(use(B_LAST, "yT_last"))
            shared_silu(1, 0)
            shared_silu(1, 1)
            shared_silu(2, 0)
            shared_silu(2, 1)
            evacuate_h2T(B_LAST, use(B_LAST, "h2T_last"))
            shared_silu(3, 0)
            exp_minus_logits(B_LAST, use(B_LAST, "lg_last"))
            shared_silu(3, 1)
            for b in range(4, B):
                for j in range(IC):
                    shared_silu(b, j)

            def unit_xT(u, slot):
                act.wait_ge(xuT_full, u + 1)
                act.activation(xuT[slot % 2], mx_bank[0][:, slot % 2, 0:P], ACT.Copy).then_inc(xuT_ready, 1)

            def unit_silu(u, slot, wait):
                act.wait_ge(gu_full, u + 1)
                if wait:
                    act.wait_ge(act_ready, u - 1)
                act.activation(silu_u[slot % 2], st_bank[slot % 2][:, 0:I], ACT.Silu).then_inc(silu_ready, 1)

            def unit_y(u, slot, turn, wait):
                act.wait_ge(yu_full, u + 1)
                if wait:
                    act.wait_ge(yu_sent[slot], 16 * turn)
                act.activation(y_u[slot], (pv_bank, misc)[slot % 2][:, 0:C], ACT.Copy, scale=w_u[slot]).then_inc(yu_ready, 1)

            def unit_step(i, k, turn, has_silu=True, has_xT=True, has_y=True, wait_silu=True, wait_y=True):
                if has_silu:
                    unit_silu(i, k % RING, wait_silu)
                if has_xT:
                    unit_xT(i + 1, (k + 1) % RING)
                if has_y:
                    unit_y(i - 2, (k - 2) % RING, turn + (k - 2) // RING, wait_y)

            unit_xT(0, 0)
            for i in range(RING + 2):
                unit_step(i, i % RING, i // RING, has_y=i >= 2, wait_silu=i >= 2, wait_y=False)
            for i in range(RING + 2, 2 * RING):
                unit_step(i, i % RING, i // RING)
            with act.Fori(2, UNITS // RING - 1) as it:
                for k in range(RING):
                    unit_step(RING * it + k, k, it)
            for i in range(UNITS - RING, UNITS + 2):
                unit_step(i, i % RING, i // RING, has_silu=i < UNITS, has_xT=i + 1 < UNITS)

        @block.vector
        def _(dve):
            dve.wait_ge(w_loaded, 64)
            dve.tensor_reduce(alpha[:], w_nat[:], AX_X, ALU.add, apply_absolute_value=True).then_inc(setup_dve, 1)
            dve.tensor_scalar(w_sgn, w_nat[:], 0.0, None, ALU.is_gt)
            dve.tensor_scalar(w_neg, w_nat[:], 0.0, None, ALU.is_lt).then_inc(setup_dve, 1)
            dve.wait_ge(setup_dve, 2)
            dve.tensor_tensor(w_sgn, w_sgn, w_neg, ALU.subtract).then_inc(setup_dve, 1)
            dve.wait_ge(setup_dve, 3)
            for i in range(4):
                dve.tensor_scalar(w_nat[:, i, :], w_sgn[:, i, :], alpha[:, i:i + 1], 1.0 / C, ALU.mult,
                                  ALU.mult).then_inc(setup_dve, 1)

            def stats(src, st, mv, chain, ready, b):
                for t in range(TT):
                    dve.bn_stats(st[:, t, :], src(t)).then_inc(chain, 1)
                for t in range(TT):
                    hold(dve, chain, TT * b.n + t + 1)
                    dve.bn_aggr(mv[:, t, :], st[:, t, :]).then_inc(ready, 1)

            def normalise(src, mv, rstd_, rstd_ready, dst, ready, b):
                dve.wait_ge(rstd_ready, b.n + 1)
                for t in range(TT):
                    dve.tensor_scalar(dst[:, t, :], src(t), mv[:, t, 0:1], rstd_[:, t:t + 1], ALU.subtract,
                                      ALU.mult).then_inc(ready, 1)

            def stats1(b):
                dve.wait_ge(x_in_loaded, 16 * (b.n + 1))
                stats(lambda t: x_in[:, t, :], stats1_sb, mv1, stats1_chain, stats1_ready, b)

            def layer_norm1(b):
                normalise(lambda t: x_in[:, t, :], mv1, rstd1, rstd1_ready, ln1, ln1_ready, b)

            def x1_tile(b):
                return lambda t: x1[:, bass.ds(TT * b.n + t, 1), :].rearrange("p o c -> p (o c)")

            def stats2(b):
                stats(x1_tile(b), stats2_sb, mv2, stats2_chain, stats2_ready, b)

            def layer_norm2(b):
                normalise(x1_tile(b), mv2, rstd2, rstd2_ready, ln2, ln2_ready, b)

            def maxima(b, g, hh, halves=(0, 1)):
                for half in halves:
                    fill = 2 * HG * (G * b.n + g) + 2 * hh + half
                    dve.wait_ge(mx_full, fill + 1)
                    dve.tensor_reduce(neg_max[g % 2][:, hh, 2 * half:2 * half + 2], mx_bank[half][:], AX_X, ALU.max,
                                      negate=True).then_inc(mx_free, 1)

            def split_max(b, g):
                grp = G * b.n + g
                nm = neg_max[g % 2][:].rearrange("p h t -> p (h t)")
                dve.wait_ge(mx_free, 2 * HG * (grp + 1))
                if b.const > 0 or g > 0:
                    dve.wait_ge(m_split, grp)
                    dve.wait_ge(m_row_loaded[(g - 1) % 2], 16 * (2 * b.n + (g - 1) // 2 + 1))
                dve.tensor_copy(m_parts[:, 0, :], nm).then_inc(m_chain, 1)
                dve.wait_ge(m_chain, 3 * grp + 1)
                dve.tensor_tensor(m_rest[:], nm, m_parts[:, 0, :], ALU.subtract).then_inc(m_chain, 1)
                dve.wait_ge(m_chain, 3 * grp + 2)
                dve.tensor_copy(m_parts[:, 1, :], m_rest[:]).then_inc(m_chain, 1)
                dve.wait_ge(m_chain, 3 * grp + 3)
                dve.tensor_tensor(m_parts[:, 2, :], m_rest[:], m_parts[:, 1, :], ALU.subtract).then_inc(m_split, 1)

            def normalise_y(b, g, done):
                y = misc[:].rearrange("p (t s d) -> p t s d", t=TT, d=32)
                dve.wait_ge(misc_full, done + 1)
                dve.reciprocal(y_rden[:], y[:, :, :, DH]).then_inc(rden_ready, 1)
                dve.wait_ge(rden_ready, G * b.n + g + 1)
                dve.tensor_tensor(y_tok[:, :, g * 32:(g + 1) * 32].rearrange("p t (s d) -> p t s d", d=DH),
                                  y[:, :, :, 0:DH], y_rden[:].unsqueeze(3).to_broadcast([P, TT, HG, DH]),
                                  ALU.mult).then_inc(misc_free, 1)

            def residual_sum(b, done):
                dve.wait_ge(xres_ready, b.n + 1)
                dve.wait_ge(misc_full, done + 1)
                dve.tensor_tensor(x1[:, bass.ds(TT * b.n, TT), :], misc[:].rearrange("p (t c) -> p t c", t=TT), x_ep[:],
                                  ALU.add).then_inc(misc_free, 1)
                hold(dve, misc_free, done + 1)

            def add_router_bias(b, done):
                dve.wait_ge(misc_full, done + 1)
                dve.tensor_tensor(logits[:], misc[:, 0:TT * E].rearrange("p (t e) -> p t e", t=TT),
                                  router_bias[:].unsqueeze(1).to_broadcast([P, TT, E]), ALU.add).then_inc(misc_free, 1)

            def link(ins, b, step, wait=True):
                ins.then_inc(route_chain, 1)
                if wait:
                    hold(dve, route_chain, CHOOSE_STEPS * b.n + step)

            def likeliest(b):
                dve.wait_ge(sig_exp, b.n + 1)
                link(dve.tensor_scalar(probs[:], probs[:], 1.0, None, ALU.add), b, 1)
                link(dve.reciprocal(probs[:], probs[:]), b, 2)
                for t in range(TT):
                    link(dve.max(top_p[:, t, :], probs[:, t, :]), b, 3 + t, wait=t == TT - 1)
                for t in range(TT):
                    link(dve.max_index(top_e[:, t, :], top_p[:, t, :], probs[:, t, :]), b, 3 + TT + t, wait=t == TT - 1)

            def choose(b):
                step = 2 + 2 * TT
                link(dve.tensor_copy(top_ef[:], top_e[:, :, 0:K_TOP]), b, step + 1, wait=False)
                link(dve.tensor_tensor(p_sum[:], top_p[:, :, 0], top_p[:, :, 1], ALU.add), b, step + 2)
                link(dve.reciprocal(p_rsum[:], p_sum[:]), b, step + 3)
                dve.wait_ge(rows_free, b.n + 1)
                for k in range(K_TOP):
                    dve.tensor_tensor(rec[b.par][:, k, :, C], top_p[:, :, k], p_rsum[:], ALU.mult).then_inc(weights_ready, 1)
                link(dve.tensor_tensor(chosen[:], expert_no[:].unsqueeze(1).unsqueeze(1).to_broadcast([P, K_TOP, TT, E]),
                                       top_ef[:].rearrange("p t k -> p k t").unsqueeze(3).to_broadcast([P, K_TOP, TT, E]),
                                       ALU.is_equal), b, CHOOSE_STEPS)
                dve.tensor_tensor(marks[:, 0:TT, :], chosen[:, 0], chosen[:, 1], ALU.add).then_inc(marks_ready, 1)

            def assign_rows(b, done):
                now, nxt = next_row[b.par], next_row[1 - b.par]
                dve.wait_ge(misc_full, done + 1)
                dve.tensor_tensor(place[:], misc[:, 0:TT * E].rearrange("p (t e) -> p t e", t=TT),
                                  now[:].unsqueeze(1).to_broadcast([P, TT, E]), ALU.add).then_inc(rank_chain, 1)
                dve.tensor_tensor(nxt[:], now[:], misc[:, TT * E:(TT + 1) * E], ALU.add).then_inc(misc_free, 1)
                dve.wait_ge(rank_chain, 3 * b.n + 1)
                dve.tensor_tensor(picked[:], chosen[:], place[:].unsqueeze(1).to_broadcast([P, K_TOP, TT, E]),
                                  ALU.mult).then_inc(rank_chain, 1)
                dve.wait_ge(rank_chain, 3 * b.n + 2)
                dve.tensor_reduce(row_f[:], picked[:], AX_X, ALU.add).then_inc(rank_chain, 1)
                dve.wait_ge(rank_chain, 3 * b.n + 3)
                dve.wait_ge(rows_free, b.n + 2)
                dve.tensor_copy(row_u[:], row_f[:]).then_inc(rows_ready, 1)

            def gate(rows, sign, step, ready):
                dve.tensor_scalar(sign, rows, 0.0, 2.0, ALU.is_ge, ALU.mult).then_inc(gate_chain, 1)
                dve.wait_ge(gate_chain, 3 * step + 1)
                dve.scalar_tensor_tensor(rows, rows, -1.0, rows, ALU.mult, ALU.max).then_inc(gate_chain, 1)
                dve.wait_ge(gate_chain, 3 * step + 2)
                dve.tensor_scalar(rows, rows, 0.25, None, ALU.max).then_inc(gate_chain, 1)
                dve.wait_ge(gate_chain, 3 * step + 3)
                dve.scalar_tensor_tensor(rows, sign, -1.0, rows, ALU.add, ALU.mult).then_inc(ready, 1)

            stats1(B0)
            layer_norm1(B0)
            fill_fixed(dve, 0)
            for i, w in enumerate("qk"):
                first_part(dve, B0, i, use(AHEAD, w + "_0"))
                split_qk(dve, B0, i)
            stats1(B1)
            layer_norm1(B1)
            for b in range(0, B, 2):
                dve.wait_ge(bc_full, b + 1)
                for k, dst in enumerate((ga_bc, sb_bc, cb_bc, gb_bc)):
                    dve.tensor_scalar(dst[:, b, :], mx_bank[(b // 2) % 2][:, b % 2, k * C:(k + 1) * C],
                                      1.0 if dst is cb_bc else 0.0, None, ALU.add).then_inc(bc_free_dve, 1)
            dve.wait_ge(bc_free_dve, 2 * B)
            dve.wait_ge(bc_free_act, 2 * B)
            gate(ga_bc[:], gate_sign, 0, gates_ready)
            for i, w in enumerate("qk"):
                first_part(dve, B1, i, use(AHEAD, w + "_1"))
                split_qk(dve, B1, i)

            for g in range(2):
                for hh in range(HG):
                    maxima(B0, g, hh)
                split_max(B0, g)

            def body(b, first, last):
                for n in range(SLOTS):
                    if n < 8 or not last:
                        maxima(*group_ahead(b, n // TT), n % TT, (0,))
                    if n == 1 and not last:
                        stats1(b.plus(2))
                    if n == 2 and not first:
                        normalise_y(b.plus(-1), G - 1, use(b, "y3"))
                    if n == 4 and not first:
                        residual_sum(b.plus(-1), use(b, "out"))
                        stats2(b.plus(-1))
                    if n == 5 and not last:
                        layer_norm1(b.plus(2))
                    if n == 7 and not first:
                        layer_norm2(b.plus(-1))
                    if n in (6, 11, 13):
                        g = (6, 11, 13).index(n)
                        normalise_y(b, g, use(b, f"y{g}"))
                    if n == 9 and not last:
                        first_part(dve, b.plus(2), 0, use(b, "q"))
                    if n == 15 and not last:
                        first_part(dve, b.plus(2), 1, use(b, "k"))
                    if n == 12 and not first:
                        add_router_bias(b.plus(-1), use(b, "lg"))
                    if n in (13, 14) and not first:
                        (likeliest, choose)[n - 13](b.plus(-1))
                    if n < 8 or not last:
                        maxima(*group_ahead(b, n // TT), n % TT, (1,))
                    if n == 15 and not first:
                        assign_rows(b.plus(-1), use(b, "rank"))
                    if n % TT == TT - 1 and (n < 8 or not last):
                        split_max(*group_ahead(b, n // TT))
                    if n in (9, 11) and last:
                        half = (n - 9) // 2
                        dve.wait_ge(parts_ready, 2 * B)
                        gate(gb_bc[:, 4 * half:4 * half + 4, :], qk_f[half][:].rearrange("p (b c) -> p b c", c=C), 1 + half, gb_ready)

            batches(dve, body)
            def shared_act(b, j):
                dve.wait_ge(s_silu, IC * b + j + 1)
                if b >= 2:
                    dve.wait_ge(s_down, b - 1)
                dve.tensor_tensor(act_s[:, b % 2, j, :], silu_s[:, j, :], mx_bank[j][:, 1, :], ALU.mult).then_inc(s_act, 1)

            def shared_sum(b):
                dve.wait_ge(s_down, b + 1)
                dve.wait_ge(gb_ready, 1 + b // 4)
                if b >= 1:
                    dve.wait_ge(s_out, b)
                dve.tensor_tensor(gated, st_bank[b % 2][:].rearrange("p (t c) -> p t c", t=TT),
                                  gb_bc[:, b:b + 1, :].to_broadcast([P, TT, C]), ALU.mult).then_inc(s_gated, 1)
                dve.wait_ge(s_gated, b + 1)
                dve.tensor_tensor(x1[:, TT * b:TT * (b + 1), :], x1[:, TT * b:TT * (b + 1), :], gated, ALU.add).then_inc(s_out, 1)

            count = [0]

            def step(ins):
                count[0] += 1
                ins.then_inc(table_chain, 1)
                dve.wait_ge(table_chain, count[0])

            def region_tables():
                used = next_row[B % 2]
                dve.wait_ge(misc_free, use(B_LAST, "rank_last") + 1)
                dve.tensor_copy(end_row[:], used[:]).then_inc(tables_ready, 1)
                step(dve.tensor_tensor(padded[:], used[:], first_row[:], ALU.subtract))
                step(dve.tensor_scalar(padded_i[:], padded[:], float(P - 1), None, ALU.add))
                shift = P.bit_length() - 1
                step(dve.tensor_scalar(padded_i[:], padded_i[:], shift, shift, ALU.logical_shift_right, ALU.logical_shift_left))
                step(dve.tensor_copy(padded[:], padded_i[:]))
                step(dve.tensor_tensor(entered[:, 0:E, :], earlier[:], padded[:].unsqueeze(1).to_broadcast([P, E, E]), ALU.mult))
                step(dve.tensor_reduce(region_end[:], entered[:, 0:E, :], AX_X, ALU.add))
                step(dve.tensor_tensor(region_end[:], region_end[:], padded[:], ALU.add))
                step(dve.tensor_scalar(skip[:], padded[:], -1.0, float(REGION), ALU.mult, ALU.add))
                step(dve.memset(skip[:, E - 1:E], float(FAR)))
                step(dve.tensor_tensor(entered[:], unit_start[:].unsqueeze(2).to_broadcast([P, UNITS, E]),
                                       region_end[:].unsqueeze(1).to_broadcast([P, UNITS, E]), ALU.is_ge))

            def unit_tables():
                step(dve.tensor_tensor(skipped[:], entered[:], skip[:].unsqueeze(1).to_broadcast([P, UNITS, E]), ALU.mult))
                step(dve.tensor_reduce(unit_f[:, 0, :], skipped[:], AX_X, ALU.add))
                step(dve.tensor_reduce(unit_f[:, 1, :], entered[:, :, 0:E - 1], AX_X, ALU.add))
                step(dve.tensor_tensor(unit_f[:, 0, :], unit_f[:, 0, :], unit_start[:], ALU.add))
                dve.tensor_scalar(unit_row[:], unit_f[:, 0, :], float(E * REGION), None, ALU.min).then_inc(tables_ready, 1)
                step(dve.tensor_tensor(digits[:], unit_f[:, 1, :].rearrange("p (g k) -> p g k", k=RING),
                                       digit[:].unsqueeze(1).to_broadcast([P, UNITS // RING, RING]), ALU.mult))
                step(dve.tensor_reduce(packed_f[:], digits[:], AX_X, ALU.add))
                dve.tensor_copy(turn_experts[:], packed_f[:]).then_inc(tables_ready, 1)

            shared_act(0, 0)
            normalise_y(B_LAST, G - 1, use(B_LAST, "y3_last"))
            shared_act(0, 1)
            shared_act(1, 0)
            residual_sum(B_LAST, use(B_LAST, "out_last"))
            stats2(B_LAST)
            shared_act(1, 1)
            shared_sum(0)
            layer_norm2(B_LAST)
            shared_act(2, 0)
            shared_act(2, 1)
            shared_sum(1)
            shared_act(3, 0)
            add_router_bias(B_LAST, use(B_LAST, "lg_last"))
            shared_act(3, 1)
            likeliest(B_LAST)
            choose(B_LAST)
            shared_act(4, 0)
            assign_rows(B_LAST, use(B_LAST, "rank_last"))
            shared_sum(2)
            shared_act(4, 1)
            region_tables()
            shared_sum(3)
            shared_act(5, 0)
            shared_act(5, 1)
            shared_sum(4)
            shared_act(6, 0)
            unit_tables()
            shared_act(6, 1)
            shared_sum(5)
            shared_act(7, 0)
            shared_act(7, 1)
            shared_sum(6)
            shared_sum(7)

            def unit_rows(u, slot, turn, wait):
                dve.wait_ge(xu_loaded[slot], 16 * (turn + 1))
                if wait:
                    dve.wait_ge(yu_sent[slot], 16 * turn)
                dve.tensor_copy(w_u[slot], xu[slot][:, C:C + 1])
                dve.tensor_copy(home_u[:, slot:slot + 1], xu[slot][:, C + 1:C + 2]).then_inc(xu_read, 1)

            def unit_act(u, slot, wait):
                dve.wait_ge(silu_ready, u + 1)
                if wait:
                    dve.wait_ge(actT_full, u - 1)
                dve.tensor_tensor(act_u[slot % 2], silu_u[slot % 2], st_bank[slot % 2][:, I:2 * I], ALU.mult).then_inc(act_ready, 1)

            def unit_actT(u, slot, wait):
                dve.wait_ge(actT_full, u + 1)
                if wait:
                    dve.wait_ge(yu_full, u - 1)
                dve.tensor_copy(actT_u[slot % 2], mx_bank[1][:, slot % 2, 0:I]).then_inc(actT_ready, 1)

            def unit_step(i, k, turn, has_rows=True, has_actT=True, has_act=True, first=False, reuse=True, wait_actT=True):
                if has_actT:
                    unit_actT(i - 1, (k - 1) % RING, wait_actT)
                if has_act:
                    unit_act(i, k % RING, not first)
                if has_rows:
                    unit_rows(i + 2, (k + 2) % RING, turn + (k + 2) // RING, reuse)

            unit_rows(0, 0, 0, False)
            unit_rows(1, 1, 0, False)
            for i in range(RING):
                unit_step(i, i, 0, has_actT=i > 0, first=i < 2, reuse=i + 2 >= RING, wait_actT=i >= 3)
            with dve.Fori(1, UNITS // RING - 1) as it:
                for k in range(RING):
                    unit_step(RING * it + k, k, it)
            for i in range(UNITS - RING, UNITS + 1):
                unit_step(i, i % RING, i // RING, has_rows=i + 2 < UNITS, has_act=i < UNITS)
            for b in range(B):
                r = results[b][0]
                xb = x1[:, TT * b:TT * (b + 1), :]
                dve.wait_ge(results_added, b + 1)
                dve.tensor_tensor(r, r, gb_bc[:, b:b + 1, :].to_broadcast([P, TT, C]), ALU.mult).then_inc(out_chain, 1)
                dve.wait_ge(out_chain, b + 1)
                dve.tensor_tensor(xb, xb, r, ALU.add).then_inc(out_ready, 1)

        @block.tensor
        def _(pe):
            def transposes(src):
                for t in range(TT):
                    last = pe.transpose(misc[:, t * P:(t + 1) * P], src(t), ident[:])
                return last

            def free(done):
                pe.wait_ge(misc_free, done)

            pe.wait_ge(consts_ready, 2)
            pe.wait_ge(setup_dve, 7)
            transposes(lambda i: w_nat[:, i, :]).then_inc(misc_full, 1)
            free(use(AHEAD, "c"))
            pe.wait_ge(c_loaded, 48)
            pe.transpose(misc[:, 0:B], c_nat[:], ident[0:B, 0:B])
            pe.transpose(misc[:, B:B + E], router_nat[:], ident[0:E, 0:E]).then_inc(misc_full, 1)
            free(use(AHEAD, "mod"))
            for j in range(2):
                last = pe.matmul(misc[:, j * B:(j + 1) * B], wmod_sb[:, j * C:(j + 1) * C], silu_T[:],
                                 start=True, stop=True)
            last.then_inc(misc_full, 1)

            def ln1_T(b, done):
                free(done)
                pe.wait_ge(ln1_ready, TT * (b.n + 1))
                transposes(lambda t: ln1[:, t, :]).then_inc(misc_full, 1)

            def project(i, done):
                free(done)
                pe.matmul(misc[:], wT[:, i, :], hT[:], start=True, stop=True).then_inc(misc_full, 1)

            def project_v(done):
                free(done)
                for t in range(TT):
                    last = pe.matmul(misc[:, t * P:(t + 1) * P], hT[:, t * P:(t + 1) * P], wT[:, 2, :],
                                     start=True, stop=True)
                last.then_inc(misc_full, 1)

            def max_T(b, g, done):
                free(done)
                hold(pe, m_split, G * b.n + g + 1)
                pe.transpose(misc_bf[0:PARTS * HG * TT, 0:P], m_parts[:].rearrange("p j m -> p (j m)"),
                             ident_bf[:]).then_inc(misc_full, 1)

            def y_T(b, g, done):
                free(done)
                pe.wait_ge(y_evacuated, G * b.n + g + 1)
                transposes(lambda t: y_strips[:, t * P:(t + 1) * P]).then_inc(misc_full, 1)

            def all_y_T(done):
                free(done)
                transposes(lambda t: y_tok[:, t, :]).then_inc(misc_full, 1)

            def project_out(b, done):
                free(done)
                pe.wait_ge(wp_ga_ready, b.n + 1)
                for t in range(TT):
                    last = pe.matmul(misc[:, t * P:(t + 1) * P], yT[:, t * P:(t + 1) * P], wp_ga[:], start=True, stop=True)
                last.then_inc(misc_full, 1)

            def h2_T(b, done):
                free(done)
                pe.wait_ge(h2_ready, K_TOP * b.n + 1)
                transposes(lambda t: rec[b.par][:, 0, t, 0:C]).then_inc(misc_full, 1)

            def router_logits(done):
                free(done)
                for t in range(TT):
                    last = pe.matmul(misc[:, t * E:(t + 1) * E], h2T_now[:, t * P:(t + 1) * P], router_T[:],
                                     start=True, stop=True)
                last.then_inc(misc_full, 1)

            def ranks(b, done):
                free(done)
                pe.wait_ge(marks_ready, b.n + 1)
                pe.matmul(misc[:, 0:(TT + 1) * E], earlier_token[:], marks[:].rearrange("p t e -> p (t e)"), start=True, stop=True)
                for t in range(TT):
                    last = pe.matmul(misc[:, (t + 1) * E:(TT + 1) * E], ones_bf[:],
                                     marks[:, t:t + 1, :].to_broadcast([P, TT - t, E]), start=False, stop=True,
                                     skip_group_check=True)
                last.then_inc(misc_full, 1)

            def max_scores(b, g, hh, half):
                h = HG * g + hh
                fill = 2 * HG * (G * b.n + g) + 2 * hh + half
                if b.const > 0 or g > 0 or hh > 0:
                    pe.wait_ge(mx_free, fill - 1)
                for t in range(2):
                    q0 = (2 * half + t) * P
                    last = pe.matmul(mx_bank[half][:, t, :], qs[b.par][0:MROW, h, q0:q0 + P], ks[b.par][0:MROW, h, :],
                                     start=True, stop=True)
                last.then_inc(mx_full, 1)

            def scores(b, n, hh):
                h, j = HG * (n // TT) + hh, n % TT
                fill = HG * (SLOTS * b.n + n) + hh
                if wide(b, n) and hh == 2 and n == SLOTS // 2:
                    pe.wait_ge(mx_free, 2 * HG * G * B)
                elif wide(b, n):
                    pe.wait_ge(exp_done, fill - HG + 1 + (n == SLOTS // 2 and hh < 2) * 2)
                elif b.const > 0 or n > 0 or hh >= 2:
                    pe.wait_ge(exp_done, fill - 1)
                pe.matmul(score_bank(b, n, hh), ks[b.par][:, h, j * P:(j + 1) * P], qs[b.par][:, h, :],
                          start=True, stop=True).then_inc(st_full, 1)

            def products(b, n):
                g, j = n // TT, n % TT
                quad = SLOTS * b.n + n
                pe.wait_ge(exp_done, HG * (quad + 1))
                if j == 0 and (b.const > 0 or g > 0):
                    pe.wait_ge(y_evacuated, G * b.n + g)
                for hh in range(HG):
                    last = pe.matmul(pv_bank[32 * hh:32 * (hh + 1), :], vs[b.par][:, j, HG * g + hh, :], pt[n % 2][:, hh, :],
                                     start=(j == 0), stop=(j == TT - 1))
                last.then_inc(pv_done, 1)

            ln1_T(B0, use(AHEAD, "ln1_0"))
            project(0, use(AHEAD, "q_0"))
            project(1, use(AHEAD, "k_0"))
            project_v(use(AHEAD, "v_0"))
            pe.wait_ge(silu_spread, 1)
            for b in range(B):
                if b >= 4:
                    pe.wait_ge((bc_free_dve, bc_free_act)[b % 2], 4 * (b // 2 - 1))
                pe.matmul(mx_bank[(b // 2) % 2][:, b % 2, :], silu_bc[:, b, :], wmod_sb[:, 2 * C:6 * C],
                          start=True, stop=True).then_inc(bc_full, 1)
            ln1_T(B1, use(AHEAD, "ln1_1"))
            project(0, use(AHEAD, "q_1"))
            project(1, use(AHEAD, "k_1"))
            free(use(AHEAD, "shared1"))
            pe.wait_ge(shared_loaded, 48)
            transposes(lambda i: nat[:, i, :]).then_inc(misc_full, 1)
            free(use(AHEAD, "shared2"))
            for j in range(IC):
                last = pe.transpose(misc[:, j * P:(j + 1) * P], nat[:, 4 + j, :], ident[:])
            last.then_inc(misc_full, 1)
            pe.wait_ge(bc_free_act, 2 * B)
            pe.wait_ge(bc_free_dve, 2 * B)
            pe.wait_ge(stack_loaded[0], STACK_DMAS)
            for g in range(2):
                for hh in range(HG):
                    for half in range(2):
                        max_scores(B0, g, hh, half)
            max_T(B0, 0, use(AHEAD, "m0"))

            def between(b, n, first, last):
                if n in (1, 5, 9):
                    max_T(b, n // 4 + 1, use(b, f"m{n // 4 + 1}"))
                if n == 2 and not first:
                    y_T(b.plus(-1), G - 1, use(b, "y3"))
                if n == 3 and not first:
                    all_y_T(use(b, "yT"))
                if n == 4 and not first:
                    project_out(b.plus(-1), use(b, "out"))
                if n == 6:
                    y_T(b, 0, use(b, "y0"))
                if n == 7 and not last:
                    ln1_T(b.plus(2), use(b, "ln1"))
                if n == 8 and not last:
                    project(0, use(b, "q"))
                if n == 10 and not first:
                    h2_T(b.plus(-1), use(b, "h2T"))
                if n == 11:
                    y_T(b, 1, use(b, "y1"))
                if n == 12 and not first:
                    router_logits(use(b, "lg"))
                if n == 13:
                    y_T(b, 2, use(b, "y2"))
                if n == 14 and not last:
                    project(1, use(b, "k"))

            def body(b, first, last):
                for n in range(SLOTS):
                    g, j = n // TT, n % TT
                    ahead = n < 8 or not last
                    ahead_b, ahead_g = group_ahead(b, g)
                    if j == 0:
                        pe.wait_ge(m_row_loaded[g % 2], 16 * (2 * b.n + g // 2 + 1))
                    if n == 8 and not last:
                        nb = b.plus(1)
                        pe.wait_ge(stack_loaded[nb.par], STACK_DMAS * (nb.half + 1))
                    scores(b, n, 0)
                    scores(b, n, 1)
                    if ahead:
                        max_scores(ahead_b, ahead_g, j, 0)
                    between(b, n, first, last)
                    scores(b, n, 2)
                    if ahead:
                        max_scores(ahead_b, ahead_g, j, 1)
                    scores(b, n, 3)
                    if n > 0:
                        products(b, n - 1)
                    elif not first:
                        products(b.plus(-1), SLOTS - 1)
                    if n == 0 and not last:
                        project_v(use(b, "v"))
                    if n == 12 and not last:
                        max_T(b.plus(1), 0, use(b, "m0"))
                    if n == 15 and not first:
                        ranks(b.plus(-1), use(b, "rank"))

            batches(pe, body)
            def shared_up(b, j):
                if b >= 1:
                    pe.wait_ge(s_act, IC * (b - 1) + j + 1)
                for which in range(2):
                    last = pe.matmul(mx_bank[j][:, which, :], shared_w[:, IC * which + j, :], h2T[:, T * b:T * (b + 1)],
                                     start=True, stop=True)
                last.then_inc(s_full, 1)

            def shared_dn(b):
                pe.wait_ge(s_act, IC * (b + 1))
                if b >= 2:
                    pe.wait_ge(s_out, b - 1)
                for t in range(TT):
                    for j in range(IC):
                        last = pe.matmul(st_bank[b % 2][:, t * P:(t + 1) * P], act_s[:, b % 2, j, t * P:(t + 1) * P],
                                         shared_down[:, j, :], start=(j == 0), stop=(j == IC - 1))
                last.then_inc(s_down, 1)

            products(B_LAST, SLOTS - 1)
            pe.wait_ge(exp_done, HG * SLOTS * B)
            shared_up(0, 0)
            y_T(B_LAST, G - 1, use(B_LAST, "y3_last"))
            shared_up(0, 1)
            all_y_T(use(B_LAST, "yT_last"))
            shared_up(1, 0)
            project_out(B_LAST, use(B_LAST, "out_last"))
            shared_up(1, 1)
            shared_dn(0)
            shared_up(2, 0)
            shared_up(2, 1)
            shared_dn(1)
            h2_T(B_LAST, use(B_LAST, "h2T_last"))
            shared_up(3, 0)
            router_logits(use(B_LAST, "lg_last"))
            shared_up(3, 1)
            shared_dn(2)
            shared_up(4, 0)
            ranks(B_LAST, use(B_LAST, "rank_last"))
            shared_up(4, 1)
            shared_dn(3)
            for b in range(5, B):
                for j in range(IC):
                    shared_up(b, j)
                shared_dn(b - 1)

            def experts_of(turn):
                return pe.value_load(turn_experts[0:1, bass.ds(turn, 1)], min_val=0, max_val=E ** RING - 1)

            def weights_of(experts, k):
                shift = E.bit_length() - 1
                return ((experts >> (shift * k)) & (E - 1)) * (IC * C)

            def ahead_of_time(value):
                return pe.snap(pe.to_reg(value), min_val=0, max_val=(E - 1) * IC * C)

            def unit_T(u, slot, turn):
                pe.wait_ge(xu_loaded[slot], 16 * (turn + 1))
                pe.transpose(mx_bank[0][:, slot % 2, 0:P], xu[slot][:, 0:C], ident[:]).then_inc(xuT_full, 1)

            def unit_up(u, slot, start):
                pe.wait_ge(xuT_ready, u + 1)
                pe.matmul(st_bank[slot % 2][:], xuT[slot % 2], gate_up[:].rearrange("p e i -> p (e i)")[:, bass.ds(2 * start, 2 * I)],
                          start=True, stop=True).then_inc(gu_full, 1)

            def unit_actT(u, slot):
                pe.wait_ge(act_ready, u + 1)
                for j in range(IC):
                    last = pe.transpose(mx_bank[1][:, slot % 2, j * P:(j + 1) * P], act_u[slot % 2][:, j * P:(j + 1) * P], ident[:])
                last.then_inc(actT_full, 1)

            def unit_dn(u, slot, start, wait):
                pe.wait_ge(actT_ready, u + 1)
                if wait:
                    pe.wait_ge(yu_ready, u - 1)
                for j in range(IC):
                    last = pe.matmul((pv_bank, misc)[slot % 2][:, 0:C], actT_u[slot % 2][:, j * P:(j + 1) * P],
                                     down[:].rearrange("p e j c -> p (e j c)")[:, bass.ds(start + j * C, C)], start=(j == 0), stop=(j == IC - 1))
                last.then_inc(yu_full, 1)

            def unit_step(i, k, turn, start, experts, has_up=True, has_T=True, has_actT=True, has_dn=True,
                          wait_dn=True, has_before=True):
                following = None
                if has_up:
                    unit_up(i, k % RING, start)
                    if k == 0 and has_before:
                        experts.append(experts_of(turn - 1))
                    if k + 1 < RING:
                        following = ahead_of_time(weights_of(experts[0], k + 1))
                if has_T:
                    unit_T(i + 1, (k + 1) % RING, turn + (k + 1) // RING)
                if has_actT:
                    unit_actT(i - 1, (k - 1) % RING)
                if has_dn:
                    unit_dn(i - 2, (k - 2) % RING, weights_of(experts[0 if k >= 2 else 1], (k - 2) % RING), wait_dn)
                return following

            pe.wait_ge(tables_ready, 3)
            experts = [experts_of(0)]
            pe.wait_ge(s_act, IC * (B - 1) + 1)
            unit_T(0, 0, 0)
            shared_dn(B - 1)
            pe.wait_ge(routed_loaded, 64)
            pe.wait_ge(s_act, IC * B)
            start = weights_of(experts[0], 0)
            for i in range(RING):
                if i < 2:
                    pe.wait_ge(s_out, B - 1 + i)
                start = unit_step(i, i, 0, start, experts, has_actT=i >= 1, has_dn=i >= 2, wait_dn=i >= 4,
                                  has_before=False)
            with pe.Fori(1, UNITS // RING - 1) as it:
                experts = [experts_of(it)]
                start = weights_of(experts[0], 0)
                for k in range(RING):
                    start = unit_step(RING * it + k, k, it, start, experts)
            experts = [experts_of(UNITS // RING - 1)]
            start = weights_of(experts[0], 0)
            for k in range(RING + 2):
                i = UNITS - RING + k
                start = unit_step(i, k, UNITS // RING - 1, start, experts, has_up=i < UNITS, has_T=i + 1 < UNITS,
                                  has_actT=i - 1 < UNITS)


_INS = ["L0_attn_x", "L0_attn_Wq", "L0_attn_bq", "L0_attn_Wk", "L0_attn_bk", "L0_attn_Wv", "L0_attn_bv",
        "L0_attn_Wp", "L0_attn_bp", "L0_ffn_shared_gate", "L0_ffn_shared_up", "L0_ffn_shared_down",
        "L0_ffn_gate_w", "L0_ffn_up_w", "L0_ffn_down_w", "L0_ffn_router_w", "L0_ffn_routing_bias",
        "L0_c", "L0_wmod"]


def kernel(**inputs):
    import numpy as np
    import concourse.bacc as bacc
    from concourse.bass_utils import run_bass_kernel_spmd

    nc = bacc.Bacc("TRN2", target_bir_lowering=False, num_devices=1)
    arrays, args = {}, []
    for name in _INS:
        a = np.ascontiguousarray(inputs[name])
        arrays[name] = a
        args.append(nc.dram_tensor(name, a.shape, mybir.dt.from_np(a.dtype), kind="ExternalInput").ap())
    out = nc.dram_tensor("out", (B, T, C), F32, kind="ExternalOutput").ap()
    adaln_block(nc, *args, out)
    return run_bass_kernel_spmd(nc, [arrays], core_ids=[0]).results[0]["out"]
```
